# Optimizing a Trainium2 kernel written in Bass

```python
import numpy as np
import jax
import jax.numpy as jnp

def _softmax(x, axis=-1):
    return jax.nn.softmax(x, axis=axis)

def _gelu(x):
    return jax.nn.gelu(x, approximate=True)

def _silu(x):
    return jax.nn.silu(x)

def _sigmoid(x):
    return jax.nn.sigmoid(x)

def _layernorm(x, axis=-1, eps=1e-05):
    m = jnp.mean(x, axis=axis, keepdims=True)
    v = jnp.var(x, axis=axis, keepdims=True)
    return (x - m) / jnp.sqrt(v + eps)

def _scatter_add(tgt, idx, src, axis=0):
    return tgt.at[idx].add(src)

def _segment_sum(src, seg, n):
    return jax.ops.segment_sum(src, seg, n)
kernel_name = 'mk_adj_resnorm_d2_adj_r2_5f7afc'

def setup_inputs(seed: int=0):
    np.random.seed(seed)
    _w = jnp.asarray

    def _rec_inputs():
        import jax
        import jax.numpy as jnp
        _gk = jax.random.key(seed)
        x = -8.776e-05 + 1 * jax.random.normal(jax.random.fold_in(_gk, 1), (4096, 256), jnp.float32)
        _w = (1.0 + jnp.arange(4096, dtype=jnp.float32)) ** (-0.5)
        _w = _w / _w.mean()
        _pij = jnp.clip(0.00390625 * _w[:, None] * _w[None, :], 0.0, 1.0)
        _a = jax.random.uniform(jax.random.fold_in(_gk, 2), (4096, 4096)) < _pij
        _a = jnp.logical_or(_a, jnp.eye(4096, dtype=bool))
        _af = _a.astype(jnp.float32)
        _af = _af * jax.random.uniform(jax.random.fold_in(_gk, 3), (4096, 4096), jnp.float32, 0.05, 1)
        adj = _af
        return (x, adj)
    x, adj = _rec_inputs()

    def _L0_gnn_setup():
        import jax, jax.numpy as jnp
        import numpy as np
        N = 5000
        IN_F = 256
        OUT_F = 256
        key = jax.random.key(seed)
        k1, k2, k3 = jax.random.split(key, 3)
        x = jax.random.normal(k1, (N, IN_F), dtype=jnp.float32)
        adj = jax.random.uniform(k2, (N, N), dtype=jnp.float32)
        stdv = 1.0 / np.sqrt(OUT_F)
        weight = jax.random.uniform(k3, (IN_F, OUT_F), dtype=jnp.float32, minval=-stdv, maxval=stdv)
        t = jnp.ones((1,), dtype=jnp.float32)
        return {'x': x, 'adj': adj, 't': t, 'weight': weight}
    _L0_gnn_all = _L0_gnn_setup()
    _L0_gnn_in = {k: v for k, v in _L0_gnn_all.items() if k in ('t', 'weight')}
    del _L0_gnn_all

    def _L1_gnn_setup():
        import jax, jax.numpy as jnp
        import numpy as np
        N = 2048
        DIM_IN = 256
        DIM_Q = 256
        DIM_K = 256
        N_GRAPHS = 32
        key = jax.random.key(seed)
        ks = jax.random.split(key, 9)
        x = jax.random.normal(ks[0], (N, DIM_IN), dtype=jnp.float32)
        b = jax.random.normal(ks[1], (N, N), dtype=jnp.float32)
        edge_encoding = jax.random.normal(ks[2], (N, N), dtype=jnp.float32)
        ptr = jnp.arange(N_GRAPHS + 1, dtype=jnp.int64) * (N // N_GRAPHS)
        s_in = 1.0 / np.sqrt(DIM_IN)
        Wq = jax.random.normal(ks[3], (DIM_Q, DIM_IN), dtype=jnp.float32) * s_in
        bq = jnp.zeros((DIM_Q,), dtype=jnp.float32)
        Wk = jax.random.normal(ks[4], (DIM_K, DIM_IN), dtype=jnp.float32) * s_in
        bk = jnp.zeros((DIM_K,), dtype=jnp.float32)
        Wv = jax.random.normal(ks[5], (DIM_K, DIM_IN), dtype=jnp.float32) * s_in
        bv = jnp.zeros((DIM_K,), dtype=jnp.float32)
        return {'x': x, 'b': b, 'edge_encoding': edge_encoding, 'ptr': ptr, 'Wq': Wq, 'bq': bq, 'Wk': Wk, 'bk': bk, 'Wv': Wv, 'bv': bv}
    _L1_gnn_all = _L1_gnn_setup()
    _L1_gnn_in = {k: v for k, v in _L1_gnn_all.items() if k in ('ptr', 'Wq', 'bq', 'Wk', 'bk', 'Wv', 'bv')}
    del _L1_gnn_all
    return {'x': x, 'adj': adj, 'L0_gnn_t': _L0_gnn_in['t'], 'L0_gnn_weight': _L0_gnn_in['weight'], 'L1_gnn_ptr': _L1_gnn_in['ptr'], 'L1_gnn_Wq': _L1_gnn_in['Wq'], 'L1_gnn_bq': _L1_gnn_in['bq'], 'L1_gnn_Wk': _L1_gnn_in['Wk'], 'L1_gnn_bk': _L1_gnn_in['bk'], 'L1_gnn_Wv': _L1_gnn_in['Wv'], 'L1_gnn_bv': _L1_gnn_in['bv']}

def reference(x, adj, L0_gnn_t, L0_gnn_weight, L1_gnn_ptr, L1_gnn_Wq, L1_gnn_bq, L1_gnn_Wk, L1_gnn_bk, L1_gnn_Wv, L1_gnn_bv):
    import jax
    import jax.numpy as jnp

    def _L0_gnn_ref(x, adj, t, weight):
        import jax, jax.numpy as jnp
        import numpy as np
        N = 5000
        IN_F = 256
        OUT_F = 256
        ts = t[0]
        support = x @ weight
        return (1.0 - ts) * support + ts * (adj @ support)

    def _L1_gnn_ref(x, b, edge_encoding, ptr, Wq, bq, Wk, bk, Wv, bv):
        import jax, jax.numpy as jnp
        import numpy as np
        N = 2048
        DIM_IN = 256
        DIM_Q = 256
        DIM_K = 256
        N_GRAPHS = 32
        n = x.shape[0]
        graph_id = jnp.searchsorted(ptr, jnp.arange(n), side='right') - 1
        mask = graph_id[:, None] == graph_id[None, :]
        query = x @ Wq.T + bq
        key = x @ Wk.T + bk
        value = x @ Wv.T + bv
        scale = 1.0 / jnp.sqrt(jnp.float32(query.shape[-1]))
        a = jnp.where(mask, query @ key.T * scale, 0.0)
        scores = (a + b + edge_encoding) * jnp.where(mask, 1.0, -1000000.0)
        softmax = jax.nn.softmax(scores, axis=-1) * mask
        return softmax @ value
    x = _layernorm(x + _L0_gnn_ref(x, adj, L0_gnn_t, L0_gnn_weight), axis=-1)
    x = _layernorm(x + _L1_gnn_ref(x, adj, adj, L1_gnn_ptr, L1_gnn_Wq, L1_gnn_bq, L1_gnn_Wk, L1_gnn_bk, L1_gnn_Wv, L1_gnn_bv), axis=-1)
    return x

_drawn_inputs = setup_inputs


def setup_inputs(seed=0):
    import zlib

    import numpy as np

    out = dict(_drawn_inputs(seed))
    spreads = {'L1_gnn_bq': (0.0, 0.8), 'L1_gnn_bk': (0.0, 2.0), 'L1_gnn_bv': (0.0, 0.1)}
    factors = {}
    for name, (base, spread) in spreads.items():
        noise = np.random.default_rng([zlib.crc32(name.encode()), seed]).standard_normal(out[name].shape)
        drawn = base * np.exp(spread * noise) if base else spread * noise
        out[name] = jnp.asarray(drawn.astype(out[name].dtype))
    for name, factor in factors.items():
        out[name] = (out[name] * factor).astype(out[name].dtype)
    return out
```

```python
from contextlib import ExitStack

import concourse.bass as bass
from concourse import mybir

F32 = mybir.dt.float32
F16 = mybir.dt.float16
BF16 = mybir.dt.bfloat16
I32 = mybir.dt.int32
ALU = mybir.AluOpType
ACT = mybir.ActivationFunctionType
AX = mybir.AxisListType

P = 128
EPS = 1e-5
BIG = 1e30
SA = 256.0
SS = 64.0
SZ = 64.0
SW = 1024.0
SK = 64.0
SQ = 256.0
SP = 1024.0
SV = 64.0


def build(nc, x, xT, adj, adjT, t, W, ptr, Wq, bq, Wk, bk, WvT, bv, out):
    N, D = x.shape
    NG = ptr.shape[0]
    T = N // P
    H = D // P
    CW = 512
    NCH = N // CW
    TG = CW // P
    RING = 4
    JB = 2
    NBLK = NCH * T // JB
    UW = N * T // NBLK
    QG = T // JB // RING
    U = N // UW
    assert U == RING and NBLK == T * U
    SMALL = 10
    MAXT = T * NCH
    NT = 3
    KS = SQ * SZ

    with ExitStack() as ctx:
        def sb(name, shape, dt):
            return ctx.enter_context(nc.sbuf_tensor(name, shape, dt))

        def sem(name):
            return ctx.enter_context(nc.semaphore(name))

        z = sb("z", [P, T, D], F32)
        zt_buf = sb("zt_buf", [P, H * 2 * N], F16)
        v_buf = sb("v_buf", [P, T * 2 * D], F16)
        s_buf = sb("s_buf", [P, (T + 1) * 2 * D], F16)
        io_buf = sb("io_buf", [P, (T + 1) * D], F32)
        w_buf = sb("w_buf", [P, RING * JB * CW + UW // 2], F32)
        gid_row = sb("gid_row", [P, N], BF16)
        zt = zt_buf[:, :].rearrange("p (k h n) -> p k h n", k=H, h=2)
        v_hl = v_buf[:, :].rearrange("p (t h d) -> p t h d", t=T, h=2)
        s_hl = s_buf[:, 0:T * 2 * D].rearrange("p (t h d) -> p t h d", t=T, h=2)
        q_hl = s_buf[:, :].rearrange("p (t k h i) -> p t k h i", t=T + 1, k=H, h=2)
        o_all = io_buf[:, :].rearrange("p (t d) -> p t d", d=D)
        x_t = v_buf[:, :].bitcast(F32).rearrange("p (k n) -> p k n", k=H)
        iota_row = zt_buf[:, 0:2 * N].bitcast(F32)
        at_or_after = zt_buf[:, 2 * N:3 * N].bitcast(BF16)
        wtmp = zt_buf[:, 3 * N:4 * N].bitcast(F32)
        wq = wtmp[:, 0:H * D].rearrange("p (k d) -> p k d", k=H)
        wk = wtmp[:, H * D:2 * H * D].rearrange("p (k d) -> p k d", k=H)
        wv = wtmp[:, 2 * H * D:3 * H * D].rearrange("p (k d) -> p k d", k=H)
        raw = [io_buf[:, s * JB * CW:(s + 1) * JB * CW].rearrange("p (j c) -> p j c", j=JB) for s in range(RING)]
        rows = [io_buf[:, RING * JB * CW + s * UW:RING * JB * CW + (s + 1) * UW] for s in range(RING)]
        ahl = [w_buf[:, s * JB * CW:(s + 1) * JB * CW].bitcast(F16).rearrange("p (h j c) -> p h j c", h=2, j=JB)
               for s in range(RING)]
        pen0 = w_buf[:, RING * JB * CW:RING * JB * CW + UW // 2].bitcast(BF16)
        adjc = [w_buf[:, s * CW:(s + 1) * CW] for s in range(4)]
        prob = [w_buf[:, (4 + s) * CW:(5 + s) * CW] for s in range(2)]
        pt = [w_buf[:, (6 + s) * CW:(7 + s) * CW].bitcast(F16) for s in range(2)]
        pen1 = w_buf[:, 8 * CW:8 * CW + CW // 2].bitcast(BF16)
        wsb = w_buf[:, 0:H * D].rearrange("p (k d) -> p k d", k=H)
        ident = sb("ident", [P, P], F32)
        ones_bf = sb("ones_bf", [P, P], BF16)
        ones_f = sb("ones_f", [P, P], F32)
        zeros_h = s_buf[:, T * 2 * D:(T + 1) * 2 * D]
        g_hl = sb("g_hl", [P, H, 2, D], F16)
        wv_hl = sb("wv_hl", [P, H, 2, D + 1], F16)
        bv_row = sb("bv_row", [P, D], F32)
        bq_c = sb("bq_c", [P, H], F32)
        bk_c = sb("bk_c", [P, H], F32)
        bqk_p = sb("bqk_p", [P, H], F32)
        kb16 = sb("kb16", [P, H], F32)
        bqk16 = sb("bqk16", [P, 1], F32)
        ptr_i = sb("ptr_i", [P, 1], I32)
        ptr_f = sb("ptr_f", [P, 1], F32)
        tcol = sb("tcol", [P, 1], F32)
        omt = sb("omt", [P, 1], F32)
        tsc0 = sb("tsc0", [P, 1], F32)
        eps_c = sb("eps_c", [P, 1], F32)
        gid_col = sb("gid_col", [P, T + 1], F32)
        nm_q = sb("nm_q", [P, NBLK], F32)
        z_q = sb("z_q", [P, NBLK], F32)
        nm_all = sb("nm_all", [P, T + 1], F32)
        z_all = sb("z_all", [P, T + 1], F32)
        c_all = sb("c_all", [P, T], F32)
        mn0 = sb("mn0", [P, 2], F32)
        stage = sb("stage", [P, TG, D], F32)
        split_f = sb("split_f", [P, 2 * CW], F32)
        bn6 = sb("bn6", [P, TG, 6], F32)
        mv = sb("mv", [P, TG, 2], F32)
        sd = sb("sd", [P, TG], F32)
        rstd = sb("rstd", [P, TG], F32)
        pre = sb("pre", [P, 2], F32)
        nnew = sb("nnew", [P, 2], F32)
        alpha = sb("alpha", [P, MAXT + 8], F32)
        rsum = sb("rsum", [P, MAXT + 8], F32)
        mvf = sb("mvf", [P, T, 2], F32)
        bnf = alpha[:, 0:6 * T].rearrange("p (t s) -> p t s", t=T)
        rstdf = sb("rstdf", [P, T], F32)
        rz = sb("rz", [P, T], F32)
        tri = stage[:, :, :].rearrange("p g d -> p (g d)").rearrange("p (i j) -> p i j", i=T)
        clo, chi, cnt, ddif, ge = (split_f[:, CW + i * T:CW + (i + 1) * T] for i in range(5))
        incl = sb("incl", [P, T], F32)
        dif = sb("dif", [P, T + 1], F32)
        tid = sb("tid", [P, NT], F32)
        code = sb("code", [P, NT], F32)
        tmp1 = sb("tmp1", [P, NT], F32)
        crow = stage[0:1, 0:2, :].rearrange("p g d -> p (g d)")[:, 0:NT * P]
        tab = stage[0:1, 2, 0:NT * P // 2 + 1].bitcast(I32)

        bank = [ctx.enter_context(nc.psum_tensor(f"bank{i}", [P, CW], F32)) for i in range(8)]

        small_in = sem("small_in")
        w_in = sem("w_in")
        xt_in = [sem(f"xt_in{i}") for i in range(8)]
        x_in = [sem(f"x_in{i}") for i in range(4)]
        const_done = sem("const_done")
        raw_in = [sem(f"raw_in{s}") for s in range(RING)]
        row_in = [sem(f"row_in{s}") for s in range(RING)]
        setup_v = sem("setup_v")
        cmp_done = sem("cmp_done")
        gid_mm = sem("gid_mm")
        gid_cp = sem("gid_cp")
        gcol_mm = sem("gcol_mm")
        bias_mm = sem("bias_mm")
        g_mm = sem("g_mm")
        weights_done = sem("weights_done")
        s_mm = sem("s_mm")
        s_hi = sem("s_hi")
        s_lo = sem("s_lo")
        s_res = sem("s_res")
        hi_done = sem("hi_done")
        lo_done = sem("lo_done")
        hl_free = sem("hl_free")
        pen_done = sem("pen_done")
        ttr_done = sem("ttr_done")
        min_done = sem("min_done")
        exp_done = sem("exp_done")
        evac = sem("evac")
        bn_done = sem("bn_done")
        mv_done = sem("mv_done")
        sd_done = sem("sd_done")
        rstd_done = sem("rstd_done")
        z_done = sem("z_done")
        z_kept = sem("z_kept")
        zt_mm = sem("zt_mm")
        zt_f = sem("zt_f")
        zt_hi = sem("zt_hi")
        zt_lo = sem("zt_lo")
        v_mm = sem("v_mm")
        v_f = sem("v_f")
        v_hi = sem("v_hi")
        v_lo = sem("v_lo")
        c_done = sem("c_done")
        table_v = sem("table_v")
        code_mm = sem("code_mm")
        table_done = sem("table_done")
        o_zero = sem("o_zero")
        state_v = sem("state_v")
        state_a = sem("state_a")
        q_mm = sem("q_mm")
        q_f = sem("q_f")
        q_hi = sem("q_hi")
        q_lo = sem("q_lo")
        adj_in = [sem(f"adj_in{s}") for s in range(4)]
        sc_mm = sem("sc_mm")
        sc_read = sem("sc_read")
        pen1_done = sem("pen1_done")
        pre_done = sem("pre_done")
        tsc_done = sem("tsc_done")
        nm_kept = sem("nm_kept")
        prob_done = sem("prob_done")
        alpha_done = sem("alpha_done")
        tr_mm = sem("tr_mm")
        pt_hi = sem("pt_hi")
        pt_lo = sem("pt_lo")
        pv_mm = sem("pv_mm")
        zsum_done = sem("zsum_done")
        o_done = sem("o_done")
        fin_v = sem("fin_v")
        x2_done = sem("x2_done")
        bnf_done = sem("bnf_done")
        var_done = sem("var_done")
        sdf_done = sem("sdf_done")
        rstdf_done = sem("rstdf_done")
        y_done = sem("y_done")
        stored = sem("stored")
        passed = sem("passed")

        block = ctx.enter_context(nc.Block())

        def wait_apart(eng, *waits):
            for s, v in waits:
                eng.wait_ge(s, v)
            eng.sem_inc(passed, 1)

        def pair_fields(eng, p):
            v = eng.value_load(tab[0:1, bass.ds(p, 1)], min_val=0, max_val=(1 << 18) - 1)
            f = []
            for k in range(2):
                chunk = (v >> (9 * k)) & (NCH - 1)
                tile = nc.s_assert_within((v >> (9 * k + 3)) & 63, 0, T,
                                          skip_runtime_bounds_check_because="the table counts at most T ends")
                f.append((eng.snap(tile), eng.snap(chunk)))
            return f

        def quads(eng):
            n = eng.value_load(tab[0:1, NT * P // 2:NT * P // 2 + 1], min_val=T - 1, max_val=MAXT - 1)
            return eng.snap(n >> 2)

        def groups(group):
            group(0, 0, True, False, False)
            group(1, 1, True, True, False)
            return group

        @block.sync
        def _(sp):
            sp.dma_start(ptr_i[0:NG, :], ptr.rearrange("(p o) -> p o", o=1)).then_inc(small_in, 16)
            sp.dma_start(tcol[:, :], t.partition_broadcast(P)).then_inc(small_in, 16)
            sp.dma_start(bv_row[:, :], bv.partition_broadcast(P)).then_inc(small_in, 16)
            sp.dma_start(bq_c[:, :], bq.rearrange("(k p) -> p k", p=P), allow_slow_non_contiguous=True).then_inc(small_in, 16)
            sp.dma_start(bk_c[:, :], bk.rearrange("(k p) -> p k", p=P), allow_slow_non_contiguous=True).then_inc(small_in, 16)
            sp.dma_start(wsb[:, :, :], W.rearrange("(k p) d -> p k d", p=P)).then_inc(w_in, 16)

            def load_xt(i):
                sp.dma_start(x_t[:, :, i * CW:(i + 1) * CW],
                             xT.rearrange("(k p) n -> p k n", p=P)[:, :, i * CW:(i + 1) * CW]).then_inc(xt_in[i], 16)

            load_xt(0)
            for dst, src in ((wq, Wq), (wk, Wk), (wv, WvT)):
                sp.dma_start(dst[:, :, :], src.rearrange("(k p) d -> p k d", p=P)).then_inc(small_in, 16)
            load_xt(1)
            for i in range(4):
                sp.dma_start(z[:, 8 * i:8 * i + 8, :],
                             x.rearrange("(t p) d -> p t d", p=P)[:, 8 * i:8 * i + 8, :]).then_inc(x_in[i], 16)
                for j in (2 * i + 2, 2 * i + 3):
                    if j < 8:
                        load_xt(j)

            def load_block(q, s):
                jb = (q & (QG - 1)) * RING + s
                sp.dma_start(raw[s], adjT[bass.ds(jb * (JB * P), JB * P), bass.ds(((q >> 2) & (NCH - 1)) * CW, CW)]
                             .rearrange("(j p) c -> p j c", p=P)).then_inc(raw_in[s], 16)

            def load_rows(q, s):
                sp.dma_start(rows[s], adj[bass.ds(q * P, P), s * UW:(s + 1) * UW]).then_inc(row_in[s], 16)

            for s in range(RING):
                load_block(0, s)
                load_rows(0, s)
            with sp.Fori(0, T - 1) as q:
                for s in range(RING):
                    wait_apart(sp, (lo_done, RING * q + s + 1))
                    load_block(q + 1, s)
                    sp.wait_ge(exp_done, RING * q + s + 1)
                    load_rows(q + 1, s)

            sp.wait_ge(table_done, 1)
            sp.wait_ge(hl_free, RING + NBLK)
            nq1 = quads(sp)
            def chunk_at(f):
                tile, chunk = f
                return sp.snap((tile & (T - 1)) * P), sp.snap(chunk * CW)

            def load_chunk(at, sl):
                sp.dma_start(adjc[sl], adj[bass.ds(at[0], P), bass.ds(at[1], CW)]).then_inc(adj_in[sl], 16)

            for k in range(2):
                f = pair_fields(sp, k)
                at = [chunk_at(x) for x in f]
                for s in range(2):
                    load_chunk(at[s], 2 * k + s)
            with sp.Fori(0, nq1) as q:
                for k in range(2):
                    f = pair_fields(sp, q * 2 + 2 + k)
                    at = [chunk_at(x) for x in f]
                    for s in range(2):
                        wait_apart(sp, (nm_kept, 4 * q + 2 * k + s + 2))
                        load_chunk(at[s], 2 * k + s)
            f = pair_fields(sp, nq1 * 2 + 2)
            at = [chunk_at(x) for x in f]
            for s in range(2):
                wait_apart(sp, (nm_kept, 4 * nq1 + s + 2))
                load_chunk(at[s], s)
            with sp.Fori(0, NCH) as g:
                sp.wait_ge(y_done, TG * (g + 1))
                sp.dma_start(out[bass.ds(g * CW, CW), :].rearrange("(t p) d -> p t d", p=P),
                             o_all[:, bass.ds(g * TG, TG), :]).then_inc(stored, 16)
            sp.wait_ge(stored, 16 * NCH)

        @block.tensor
        def _(pe):
            mm = nc.tensor.matmul
            pe.wait_ge(const_done, 1)
            pe.wait_ge(cmp_done, 1)
            for i in range(NCH):
                if i >= 2:
                    pe.wait_ge(gid_cp, i - 1)
                mm(bank[4 + i % 2][:, :], ones_bf[:, :], at_or_after[:, i * CW:(i + 1) * CW],
                   start=True, stop=True).then_inc(gid_mm, 1)
            for i in range(T):
                last = mm(bank[6][:, i:i + 1], at_or_after[:, i * P:(i + 1) * P], ones_bf[:, 0:1],
                          start=True, stop=True)
            last.then_inc(gcol_mm, 1)
            pe.wait_ge(w_in, 16)
            for i in range(T):
                if i % TG == 0:
                    pe.wait_ge(xt_in[i // TG], 16)
                if i >= 4:
                    pe.wait_ge(s_hi, i - 3)
                    pe.wait_ge(s_lo, i - 3)
                    pe.wait_ge(s_res, i - 3)
                for k in range(H):
                    last = mm(bank[i % 4][:, 0:D], x_t[:, k, i * P:(i + 1) * P], wsb[:, k, :],
                              start=(k == 0), stop=(k == H - 1))
                last.then_inc(s_mm, 1)
                if i == 8:
                    pe.wait_ge(small_in, 16 * 8)
                    pe.wait_ge(setup_v, 2)
                    for f in range(H):
                        for k in range(H):
                            mm(bank[6][:, 64 + f:65 + f], wk[:, k, f * P:(f + 1) * P], bq_c[:, k:k + 1],
                               start=(k == 0), stop=(k == H - 1))
                    for f in range(H):
                        for k in range(H):
                            mm(bank[6][:, 68 + f:69 + f], wq[:, k, f * P:(f + 1) * P], bk_c[:, k:k + 1],
                               start=(k == 0), stop=(k == H - 1))
                    for k in range(H):
                        last = mm(bank[6][:, 72:73], ones_f[:, :], bqk_p[:, k:k + 1],
                                  start=(k == 0), stop=(k == H - 1))
                    last.then_inc(bias_mm, 1)
                    for f in range(H):
                        for k in range(H):
                            last = mm(bank[7][:, f * D:(f + 1) * D], wq[:, k, f * P:(f + 1) * P], wk[:, k, :],
                                      start=(k == 0), stop=(k == H - 1))
                    last.then_inc(g_mm, 1)
            pe.wait_ge(s_lo, T)
            pe.wait_ge(s_res, T)
            pe.sem_inc(hl_free, RING)

            def layer0_quad(g, acc, n):
                for s in range(RING):
                    pe.wait_ge(lo_done, (g * QG + n) * RING + s + 1)
                    for j in range(JB):
                        jt = (n * RING + s) * JB + j
                        for i in range(TG):
                            dst = bank[acc + i // 2][:, (i % 2) * D:(i % 2 + 1) * D]
                            for a, b in ((0, 0), (0, 1), (1, 0)):
                                last = mm(dst, ahl[s][:, a, j, i * P:(i + 1) * P],
                                          s_hl[:, bass.ds(jt, 1), b, :].rearrange("p o d -> p (o d)"),
                                          start=False, stop=False, skip_group_check=True)
                    last.then_inc(hl_free, 1)

            def turn_z(g):
                pe.wait_ge(z_done, TG * (g + 1))
                pe.wait_ge(v_f, TG * g)
                for k in range(H):
                    for i in range(TG):
                        last = nc.tensor.transpose(bank[4 + k][:, i * P:(i + 1) * P],
                                                   stage[:, i, k * P:(k + 1) * P], ident[:, :])
                last.then_inc(zt_mm, 1)

            def project_v(g):
                pe.wait_ge(weights_done, 4)
                pe.wait_ge(zt_lo, H * (g + 1))
                for i in range(TG):
                    n = 0
                    for k in range(H):
                        for a, b in ((0, 0), (0, 1), (1, 0)):
                            last = mm(bank[4 + i][:, 0:D + 1], zt[:, k, a, bass.ds((g * TG + i) * P, P)],
                                      wv_hl[:, k, b, :], start=(n == 0), stop=(n == 3 * H - 1))
                            n += 1
                    last.then_inc(v_mm, 1)

            def group(g, par, main, post1, post2):
                acc = 2 * par
                if main:
                    if isinstance(g, int) and g < 2:
                        pass
                    else:
                        pe.wait_ge(evac, TG * (g - 1))
                    for a in range(2):
                        mm(bank[acc + a][:, :], zeros_h[:, 0:P], zeros_h, start=True, stop=False,
                           skip_group_check=True)
                    with pe.Fori(0, 2) as n:
                        layer0_quad(g, acc, n)
                if post1:
                    turn_z(g - 1)
                if main:
                    with pe.Fori(2, QG) as n:
                        layer0_quad(g, acc, n)
                if post1:
                    project_v(g - 1)

            groups(group)
            with pe.Fori(1, NCH // 2) as gp:
                group(gp * 2, 0, True, True, True)
                group(gp * 2 + 1, 1, True, True, True)
            group(NCH, 0, False, True, True)

            pe.wait_ge(table_v, 1)
            for h in range(NT):
                last = mm(bank[0][0:1, h * P:(h + 1) * P], code[:, h:h + 1], ident[:, :], start=True, stop=True)
            last.then_inc(code_mm, 1)

            pe.wait_ge(v_f, TG * NCH)
            with pe.Fori(0, NCH // 2) as gp:
                for e in range(2):
                    for f in range(H):
                        i = 2 * e + f
                        pe.wait_ge(q_hi, 4 * gp + i + 1)
                        n = 0
                        for k in range(H):
                            for a, b in ((0, 0), (0, 1), (1, 0)):
                                last = mm(bank[4 + i][:, :], g_hl[:, k, a, f * P:(f + 1) * P],
                                          zt[:, k, b, bass.ds((gp * 2 + e) * CW, CW)],
                                          start=(n == 0), stop=(n == 3 * H - 1))
                                n += 1
                        last.then_inc(q_mm, 1)

            def scores(f, s, tt):
                tile, chunk = f
                if not isinstance(tt, int):
                    pe.wait_ge(sc_read, tt - 1)
                n = 0
                for k in range(H):
                    for a, b in ((0, 0), (0, 1), (1, 0)):
                        last = mm(bank[s][:, :], q_hl[:, bass.ds(tile, 1), k, a, :].rearrange("p o i -> p (o i)"),
                                  zt[:, k, b, bass.ds(chunk * CW, CW)], start=(n == 0), stop=(n == 3 * H - 1))
                        n += 1
                last.then_inc(sc_mm, 1)

            pe.wait_ge(table_done, 1)
            pe.wait_ge(q_lo, 2 * NCH + 2)
            nq1 = quads(pe)
            f = pair_fields(pe, 0)
            scores(f[0], 0, 0)
            scores(f[1], 1, 1)
            with pe.Fori(0, nq1 + 1) as q:
                now = pair_fields(pe, q * 2)
                for k in range(2):
                    ahead = pair_fields(pe, q * 2 + k + 1)
                    for s in range(2):
                        tt = 4 * q + 2 * k + s
                        pe.wait_ge(prob_done, tt + 1)
                        pe.wait_ge(pt_lo, tt + 1)
                        for c in range(TG):
                            last = nc.tensor.transpose(bank[2 + s][:, c * P:(c + 1) * P],
                                                       prob[s][:, c * P:(c + 1) * P], ident[:, :])
                        last.then_inc(tr_mm, 1)
                        scores(ahead[s], s, tt + 2)
                        pe.wait_ge(pt_lo, tt + 3)
                        pe.wait_ge(o_done, tt + 1)
                        n = 0
                        for c in range(TG):
                            for a, b in ((0, 0), (0, 1), (1, 0)):
                                last = mm(bank[6 + s][:, 0:D], pt[s][:, a * CW + c * P:a * CW + (c + 1) * P],
                                          v_hl[:, bass.ds(now[s][1] * TG + c, 1), b, :].rearrange("p o d -> p (o d)"),
                                          start=(n == 0), stop=(n == 3 * TG - 1))
                                n += 1
                        last.then_inc(pv_mm, 1)
                    now = ahead

        @block.scalar
        def _(act):
            A = nc.scalar.activation
            for i in range(NCH):
                act.wait_ge(gid_mm, i + 1)
                A(gid_row[:, i * CW:(i + 1) * CW], bank[4 + i % 2][:, :], ACT.Copy).then_inc(gid_cp, 1)
            for i in range(T):
                act.wait_ge(s_res, i + 1)
                A(s_hl[:, i, 0, :], bank[i % 4][:, 0:D], ACT.Copy, scale=SS).then_inc(s_hi, 1)

            def quad(g, n):
                q = g * QG + n
                for s in range(RING):
                    b = RING * q + s
                    act.wait_ge(raw_in[s], 16 * (q + 1))
                    act.wait_ge(hl_free, b + 1)
                    A(ahl[s][:, 0, :, :], raw[s], ACT.Copy, scale=SA).then_inc(hi_done, 1)
                    if not isinstance(b, int) or b >= 2:
                        sums(b - 2, (s - 2) % RING)

            def sums(b, s):
                act.wait_ge(min_done, b + 1)
                A(rows[s], rows[s], ACT.Exp, bias=nm_q[:, bass.ds(b, 1)], scale=-1.0,
                  accum_out=z_q[:, bass.ds(b, 1)]).then_inc(exp_done, 1)

            def spread(g):
                act.wait_ge(mv_done, TG * (g + 1))
                A(sd[:, :], mv[:, :, 1], ACT.Sqrt, bias=eps_c[:, :]).then_inc(sd_done, 1)

            def keep_zt(g):
                act.wait_ge(zt_mm, g + 1)
                for k in range(H):
                    act.wait_ge(v_lo, TG * g)
                    A(split_f[:, k * CW:(k + 1) * CW], bank[4 + k][:, :], ACT.Copy, scale=SZ).then_inc(zt_f, 1)
                    A(zt[:, k, 0, bass.ds(g * CW, CW)], bank[4 + k][:, :], ACT.Copy, scale=SZ).then_inc(zt_hi, 1)

            def keep_v(g):
                for i in range(TG):
                    act.wait_ge(v_f, TG * g + i + 1)
                    A(v_hl[:, bass.ds(g * TG + i, 1), 0, :].rearrange("p o d -> p (o d)"),
                      split_f[:, i * D:(i + 1) * D], ACT.Copy).then_inc(v_hi, 1)

            def group(g, par, main, post1, post2):
                if main:
                    quad(g, 0)
                if post1:
                    spread(g - 1)
                if main:
                    quad(g, 1)
                if post2:
                    keep_v(g - 2)
                if main:
                    quad(g, 2)
                if post1:
                    keep_zt(g - 1)
                if main:
                    quad(g, 3)

            groups(group)
            with act.Fori(1, NCH // 2) as gp:
                group(gp * 2, 0, True, True, True)
                group(gp * 2 + 1, 1, True, True, True)
            sums(NBLK - 2, RING - 2)
            sums(NBLK - 1, RING - 1)
            group(NCH, 0, False, True, True)
            group(NCH + 1, 1, False, False, True)

            act.wait_ge(state_v, 2)
            A(nm_q[:, :], nm_q[:, :], ACT.Exp).then_inc(state_a, 1)

            act.sem_inc(q_hi, 4)
            act.wait_ge(v_lo, T)
            with act.Fori(0, NCH // 2) as gp:
                for e in range(2):
                    for f in range(H):
                        i = 2 * e + f
                        act.wait_ge(q_mm, 4 * gp + i + 1)
                        act.wait_ge(q_lo, 4 * gp + i + 1)
                        buf = split_f[:, f * CW:(f + 1) * CW]
                        A(buf, bank[4 + i][:, :], ACT.Identity, bias=kb16[:, f:f + 1],
                          scale=SQ / 16 / (SW * SZ)).then_inc(q_f, 1)
                        act.wait_ge(q_f, 4 * gp + i + 1)
                        A(q_hl[:, bass.ds((gp * 2 + e) * TG, TG), f, 0, :], buf.rearrange("p (t i) -> p t i", t=TG),
                          ACT.Copy).then_inc(q_hi, 1)

            def soften(tt, s):
                act.wait_ge(tsc_done, tt + 1)
                A(prob[s], prob[s], ACT.Exp, bias=nnew[:, s:s + 1], scale=-1.0,
                  accum_out=rsum[:, bass.ds(tt, 1)]).then_inc(prob_done, 1)
                A(alpha[:, bass.ds(tt, 1)], pre[:, s:s + 1], ACT.Exp, bias=nnew[:, s:s + 1],
                  scale=-1.0).then_inc(alpha_done, 1)

            act.wait_ge(table_done, 1)
            nq1 = quads(act)
            act.sem_inc(tr_mm, 2)
            soften(0, 0)
            soften(1, 1)
            with act.Fori(0, nq1 + 1) as q:
                for k in range(4):
                    s = k % 2
                    tt = 4 * q + k
                    act.wait_ge(tr_mm, tt + 3)
                    act.wait_ge(pv_mm, tt + 1)
                    A(pt[s][:, 0:CW], bank[2 + s][:, :], ACT.Copy, scale=SP).then_inc(pt_hi, 1)
                    soften(tt + 2, s)

            act.wait_ge(var_done, 1)
            A(rstdf[:, :], mvf[:, :, 1], ACT.Sqrt, bias=eps_c[:, :]).then_inc(sdf_done, 1)

        @block.gpsimd
        def _(pool):
            nc.gpsimd.iota(iota_row, [[1, N]], base=0, channel_multiplier=0,
                           allow_small_or_imprecise_dtypes=True).then_inc(const_done, 1)
            nc.gpsimd.memset(ident[:, :], 0.0).then_inc(const_done, 1)
            pool.wait_ge(const_done, 2)
            nc.gpsimd.affine_select(out=ident[:, :], in_=ident[:, :], compare_op=ALU.not_equal, fill=1.0, base=0,
                                    pattern=[[-1, P]], channel_multiplier=1).then_inc(const_done, 1)
            nc.gpsimd.memset(zeros_h, 0.0).then_inc(const_done, 1)
            nc.gpsimd.memset(tri[:, :, :], 1.0).then_inc(const_done, 1)
            pool.wait_ge(const_done, 5)
            nc.gpsimd.affine_select(out=tri[:, :, :], in_=tri[:, :, :], compare_op=ALU.is_ge, fill=0.0, base=0,
                                    pattern=[[1, T], [-1, T]], channel_multiplier=0).then_inc(const_done, 1)
            nc.gpsimd.iota(tid[:, :], [[P, NT]], base=0, channel_multiplier=1,
                           allow_small_or_imprecise_dtypes=True).then_inc(const_done, 1)

            def keep_z(g):
                pool.wait_ge(z_done, TG * (g + 1))
                nc.gpsimd.tensor_copy(z[:, bass.ds(g * TG, TG), :], stage[:, :, :]).then_inc(z_kept, 1)

            def zt_low(g):
                for k in range(H):
                    pool.wait_ge(zt_hi, H * g + k + 1)
                    nc.gpsimd.tensor_tensor(zt[:, k, 1, bass.ds(g * CW, CW)], split_f[:, k * CW:(k + 1) * CW],
                                            zt[:, k, 0, bass.ds(g * CW, CW)], ALU.subtract).then_inc(zt_lo, 1)

            def v_low(g):
                for i in range(TG):
                    pool.wait_ge(v_hi, TG * g + i + 1)
                    nc.gpsimd.tensor_tensor(v_hl[:, bass.ds(g * TG + i, 1), 1, :].rearrange("p o d -> p (o d)"),
                                            split_f[:, i * D:(i + 1) * D],
                                            v_hl[:, bass.ds(g * TG + i, 1), 0, :].rearrange("p o d -> p (o d)"),
                                            ALU.subtract).then_inc(v_lo, 1)

            with pool.Fori(0, NCH) as g:
                keep_z(g)
                zt_low(g)
                v_low(g)
            pool.wait_ge(exp_done, NBLK)
            pool.wait_ge(lo_done, NBLK)
            nc.gpsimd.memset(o_all[:, :, :], 0.0).then_inc(o_zero, 1)
            pool.sem_inc(q_lo, 2)
            with pool.Fori(0, NCH) as g:
                for f in range(H):
                    pool.wait_ge(q_hi, 2 * g + f + 5)
                    nc.gpsimd.tensor_tensor(q_hl[:, bass.ds(g * TG, TG), f, 1, :],
                                            split_f[:, f * CW:(f + 1) * CW].rearrange("p (t i) -> p t i", t=TG),
                                            q_hl[:, bass.ds(g * TG, TG), f, 0, :], ALU.subtract).then_inc(q_lo, 1)

        @block.vector
        def _(dve):
            V = nc.vector
            chain = [0]

            def step(ins):
                chain[0] += 1
                ins.then_inc(fin_v, 1)
                dve.wait_ge(fin_v, chain[0])

            V.memset(ones_bf[:, :], 1.0)
            V.memset(ones_f[:, :], 1.0)
            V.memset(eps_c[:, :], EPS)
            V.memset(gid_col[:, T:T + 1], -1.0)
            V.memset(z_all[:, T:T + 1], 0.0)
            V.memset(nm_all[:, T:T + 1], 0.0)
            V.memset(ddif[:, T - 1:T], 0.0)
            step(V.memset(ptr_f[:, :], 1e9))
            dve.wait_ge(small_in, 16 * 8)
            step(V.tensor_copy(ptr_f[0:NG, :], ptr_i[0:NG, :]))
            dve.wait_ge(const_done, 7)
            V.tensor_scalar(at_or_after, iota_row, ptr_f[:, 0:1], None, ALU.is_ge).then_inc(cmp_done, 1)
            step(V.tensor_scalar(omt[:, :], tcol[:, :], -1.0, 1.0, ALU.mult, ALU.add))
            step(V.tensor_scalar(tsc0[:, :], tcol[:, :], 1.0 / (SA * SS), None, ALU.mult))
            V.tensor_tensor(bqk_p[:, :], bq_c[:, :], bk_c[:, :], ALU.mult).then_inc(setup_v, 1)
            step(V.tensor_scalar(bv_row[:, :], bv_row[:, :], SV, None, ALU.mult))
            dve.wait_ge(gcol_mm, 1)
            V.tensor_copy(gid_col[:, 0:T], bank[6][:, 0:T]).then_inc(setup_v, 1)

            def residual(i):
                dve.wait_ge(s_mm, i + 1)
                if i % 8 == 0:
                    dve.wait_ge(x_in[i // 8], 16)
                V.scalar_tensor_tensor(out=z[:, i, :], in0=bank[i % 4][:, 0:D], scalar=omt[:, 0:1],
                                       in1=z[:, i, :], op0=ALU.mult, op1=ALU.add).then_inc(s_res, 1)

            def low(i):
                dve.wait_ge(s_hi, i + 1)
                V.scalar_tensor_tensor(out=s_hl[:, i, 1, :], in0=bank[i % 4][:, 0:D], scalar=SS,
                                       in1=s_hl[:, i, 0, :], op0=ALU.mult, op1=ALU.subtract).then_inc(s_lo, 1)

            for i in range(T):
                residual(i)
                if i:
                    low(i - 1)
            low(T - 1)
            dve.wait_ge(bias_mm, 1)
            dve.wait_ge(g_mm, 1)
            step(V.tensor_scalar(kb16[:, :], bank[6][:, 64:64 + H], SQ / 16, None, ALU.mult))
            step(V.tensor_scalar(bqk16[:, :], bank[6][:, 72:73], 1.0 / 16, None, ALU.mult))
            step(V.tensor_scalar(wv_hl[:, :, 0, 0:D], wv[:, :, :], SW, None, ALU.mult))
            V.scalar_tensor_tensor(out=wv_hl[:, :, 1, 0:D], in0=wv[:, :, :], scalar=SW, in1=wv_hl[:, :, 0, 0:D],
                                   op0=ALU.mult, op1=ALU.subtract).then_inc(weights_done, 1)
            for k in range(H):
                step(V.tensor_scalar(wv_hl[:, k, 0, D:D + 1], bank[6][:, 68 + k:69 + k], SK, None, ALU.mult))
                V.scalar_tensor_tensor(out=wv_hl[:, k, 1, D:D + 1], in0=bank[6][:, 68 + k:69 + k], scalar=SK,
                                       in1=wv_hl[:, k, 0, D:D + 1], op0=ALU.mult,
                                       op1=ALU.subtract).then_inc(weights_done, 1)
            gps = bank[7][:, :].rearrange("p (k d) -> p k d", k=H)
            step(V.tensor_scalar(g_hl[:, :, 0, :], gps, SW, None, ALU.mult))
            V.scalar_tensor_tensor(out=g_hl[:, :, 1, :], in0=gps, scalar=SW, in1=g_hl[:, :, 0, :],
                                   op0=ALU.mult, op1=ALU.subtract).then_inc(weights_done, 1)

            def quad(g, n):
                q = g * QG + n
                for s in range(RING):
                    b = RING * q + s
                    dve.wait_ge(hi_done, b + 1)
                    V.scalar_tensor_tensor(out=ahl[s][:, 1, :, :], in0=raw[s], scalar=SA, in1=ahl[s][:, 0, :, :],
                                           op0=ALU.mult, op1=ALU.subtract).then_inc(lo_done, 1)
                    before = not isinstance(b, int) or b >= 1
                    if before:
                        dve.wait_ge(ttr_done, b)
                    V.tensor_scalar(pen0, gid_row[:, s * UW:(s + 1) * UW], gid_col[:, bass.ds(q, 1)], BIG,
                                    ALU.is_equal, ALU.mult).then_inc(pen_done, 1)
                    if before:
                        keep_min(b - 1, (s - 1) % 2)
                    wait_apart(dve, (pen_done, b + 1), (row_in[s], 16 * (q + 1)))
                    V.tensor_tensor_reduce(rows[s], rows[s], pen0, 2e6, 3e38, ALU.add, ALU.min,
                                           mn0[:, s % 2:s % 2 + 1]).then_inc(ttr_done, 1)

            def keep_min(b, m):
                V.tensor_scalar(nm_q[:, bass.ds(b, 1)], mn0[:, m:m + 1], 1.0, None, ALU.mult).then_inc(min_done, 1)

            def take(g, par):
                dve.wait_ge(hl_free, RING + (g + 1) * QG * RING)
                dve.wait_ge(zt_mm, g)
                dve.wait_ge(z_kept, g)
                for i in range(TG):
                    V.scalar_tensor_tensor(out=stage[:, i, :], in0=bank[2 * par + i // 2][:, (i % 2) * D:(i % 2 + 1) * D],
                                           scalar=tsc0[:, 0:1],
                                           in1=z[:, bass.ds(g * TG + i, 1), :].rearrange("p o d -> p (o d)"),
                                           op0=ALU.mult, op1=ALU.add).then_inc(evac, 1)
                for i in range(TG):
                    dve.wait_ge(evac, TG * g + i + 1)
                    V.bn_stats(bn6[:, i, :], stage[:, i, :]).then_inc(bn_done, 1)
                for i in range(TG):
                    wait_apart(dve, (bn_done, TG * g + i + 1))
                    V.bn_aggr(mv[:, i, :], bn6[:, i, :]).then_inc(mv_done, 1)

            def normalise(g):
                dve.wait_ge(sd_done, g + 1)
                V.reciprocal(rstd[:, :], sd[:, :]).then_inc(rstd_done, 1)
                dve.wait_ge(rstd_done, g + 1)
                for i in range(TG):
                    V.tensor_scalar(stage[:, i, :], stage[:, i, :], mv[:, i, 0:1], rstd[:, i:i + 1],
                                    ALU.subtract, ALU.mult).then_inc(z_done, 1)

            def take_v(g):
                dve.wait_ge(zt_lo, H * (g + 1))
                for i in range(TG):
                    dve.wait_ge(v_mm, TG * g + i + 1)
                    V.tensor_scalar(c_all[:, bass.ds(g * TG + i, 1)], bank[4 + i][:, D:D + 1],
                                    1.0 / (SZ * SK * 16), bqk16[:, 0:1], ALU.mult, ALU.add).then_inc(c_done, 1)
                    V.scalar_tensor_tensor(out=split_f[:, i * D:(i + 1) * D], in0=bank[4 + i][:, 0:D],
                                           scalar=SV / (SZ * SW), in1=bv_row[:, :], op0=ALU.mult,
                                           op1=ALU.add).then_inc(v_f, 1)

            def group(g, par, main, post1, post2):
                if main:
                    quad(g, 0)
                if post1:
                    take(g - 1, 1 - par)
                if post2:
                    take_v(g - 2)
                if main:
                    quad(g, 1)
                if post1:
                    normalise(g - 1)
                if main:
                    quad(g, 2)
                    quad(g, 3)

            group(0, 0, True, False, False)
            first = gid_row[:, :].rearrange("p (t i) -> p t i", i=P)[:, :, 0:1].to_broadcast([P, T, NCH])
            last_ = gid_row[:, :].rearrange("p (t i) -> p t i", i=P)[:, :, P - 1:P].to_broadcast([P, T, NCH])
            cfirst = gid_row[:, :].rearrange("p (o c i) -> p o c i", o=1, i=CW)[:, :, :, 0].to_broadcast([P, T, NCH])
            clast = gid_row[:, :].rearrange("p (o c i) -> p o c i", o=1, i=CW)[:, :, :, CW - 1].to_broadcast([P, T, NCH])
            cmp = split_f[:, 0:T * NCH].rearrange("p (t c) -> p t c", t=T)
            step(V.tensor_tensor(cmp, clast, first, ALU.is_lt))
            step(V.tensor_reduce(clo, cmp, AX.X, ALU.add))
            step(V.tensor_tensor(cmp, cfirst, last_, ALU.is_le))
            step(V.tensor_reduce(chi, cmp, AX.X, ALU.add))
            step(V.tensor_tensor(cnt, chi, clo, ALU.subtract))
            step(V.tensor_tensor(tri[:, :, :], tri[:, :, :],
                                 cnt.rearrange("p (o t) -> p o t", o=1).to_broadcast([P, T, T]), ALU.mult))
            step(V.tensor_reduce(incl[:, :], tri[:, :, :], AX.X, ALU.add))
            step(V.tensor_tensor(dif[:, 0:T], chi, incl[:, :], ALU.subtract))
            step(V.tensor_tensor(ddif[:, 0:T - 1], dif[:, 1:T], dif[:, 0:T - 1], ALU.subtract))
            for h in range(NT):
                step(V.tensor_scalar(ge, incl[:, :], tid[:, h:h + 1], None, ALU.is_le))
                step(V.tensor_reduce(code[:, h:h + 1], ge, AX.X, ALU.add))
                step(V.tensor_tensor(ge, ge, ddif[:, :], ALU.mult))
                step(V.tensor_reduce(tmp1[:, h:h + 1], ge, AX.X, ALU.add))
            step(V.scalar_tensor_tensor(out=tmp1[:, :], in0=tmp1[:, :], scalar=dif[:, 0:1], in1=tid[:, :],
                                        op0=ALU.add, op1=ALU.add))
            step(V.scalar_tensor_tensor(out=tmp1[:, :], in0=code[:, :], scalar=T - 0.5, in1=tmp1[:, :],
                                        op0=ALU.is_lt, op1=ALU.mult))
            V.scalar_tensor_tensor(out=code[:, :], in0=code[:, :], scalar=8.0, in1=tmp1[:, :],
                                   op0=ALU.mult, op1=ALU.add).then_inc(table_v, 1)

            group(1, 1, True, True, False)
            with dve.Fori(1, NCH // 2) as gp:
                group(gp * 2, 0, True, True, True)
                group(gp * 2 + 1, 1, True, True, True)
            dve.wait_ge(ttr_done, NBLK)
            keep_min(NBLK - 1, 1)
            group(NCH, 0, False, True, True)
            group(NCH + 1, 1, False, False, True)

            dve.wait_ge(code_mm, 1)
            dve.wait_ge(z_kept, NCH)
            step(V.tensor_copy(crow, bank[0][0:1, 0:NT * P]))
            pairs = crow.rearrange("p (t e) -> p t e", e=2)
            V.scalar_tensor_tensor(out=tab[:, 0:NT * P // 2], in0=pairs[:, :, 1], scalar=512.0, in1=pairs[:, :, 0],
                                   op0=ALU.mult, op1=ALU.add)
            step(V.tensor_scalar(tab[:, NT * P // 2:], incl[0:1, T - 1:T], -1.0, None, ALU.add))
            dve.sem_inc(table_done, 1)

            dve.wait_ge(exp_done, NBLK)
            dve.wait_ge(min_done, NBLK)
            units = nm_q[:, :].rearrange("p (t u) -> p t u", u=U)
            sums = z_q[:, :].rearrange("p (t u) -> p t u", u=U)
            V.tensor_reduce(nm_all[:, 0:T], units, AX.X, ALU.min).then_inc(state_v, 1)
            dve.wait_ge(state_v, 1)
            V.tensor_tensor(units, nm_all[:, 0:T].rearrange("p (t o) -> p t o", o=1).to_broadcast([P, T, U]), units,
                            ALU.subtract).then_inc(state_v, 1)
            dve.wait_ge(state_a, 1)
            step(V.tensor_tensor(z_q[:, :], z_q[:, :], nm_q[:, :], ALU.mult))
            V.tensor_reduce(z_all[:, 0:T], sums, AX.X, ALU.add)
            dve.wait_ge(c_done, T)
            step(V.tensor_tensor(nm_all[:, 0:T], nm_all[:, 0:T], c_all[:, :], ALU.add))

            def score(f, tt, sl, q):
                tile, chunk = f
                s = sl % 2
                dve.wait_ge(sc_mm, tt + 1)
                dve.wait_ge(adj_in[sl], 16 * (q + 1))
                V.scalar_tensor_tensor(out=adjc[sl], in0=adjc[sl], scalar=-2.0 * KS, in1=bank[s][:, :],
                                       op0=ALU.mult, op1=ALU.subtract).then_inc(sc_read, 1)
                V.tensor_scalar(pen1, gid_row[:, bass.ds(chunk * CW, CW)], gid_col[:, bass.ds(tile, 1)], BIG,
                                ALU.not_equal, ALU.mult).then_inc(pen1_done, 1)
                dve.wait_ge(nm_kept, tt + 1)
                V.tensor_scalar(pre[:, s:s + 1], nm_all[:, bass.ds(tile, 1)], 1.0, None, ALU.mult).then_inc(pre_done, 1)
                wait_apart(dve, (pre_done, tt + 1), (pen1_done, tt + 1), (sc_read, tt + 1), (tr_mm, tt + 1))
                V.tensor_tensor_reduce(prob[s], adjc[sl], pen1, 1.0 / KS, pre[:, s:s + 1], ALU.add, ALU.min,
                                       nnew[:, s:s + 1]).then_inc(tsc_done, 1)
                dve.wait_ge(tsc_done, tt + 1)
                V.tensor_scalar(nm_all[:, bass.ds(tile, 1)], nnew[:, s:s + 1], 1.0, None, ALU.mult).then_inc(nm_kept, 1)

            def gather(f, tt, s):
                tile = f[0]
                al = alpha[:, bass.ds(tt, 1)]
                dve.wait_ge(alpha_done, tt + 1)
                dve.wait_ge(zsum_done, tt + 1)
                V.scalar_tensor_tensor(out=z_all[:, bass.ds(tile, 1)], in0=z_all[:, bass.ds(tile, 1)], scalar=al,
                                       in1=rsum[:, bass.ds(tt, 1)], op0=ALU.mult, op1=ALU.add).then_inc(zsum_done, 1)
                dve.wait_ge(pv_mm, tt + 3)
                dve.wait_ge(o_done, tt + 2)
                o = o_all[:, bass.ds(tile, 1), :].rearrange("p o d -> p (o d)")
                V.scalar_tensor_tensor(out=o, in0=o, scalar=al, in1=bank[6 + s][:, 0:D],
                                       op0=ALU.mult, op1=ALU.add).then_inc(o_done, 1)

            dve.wait_ge(o_zero, 1)
            dve.sem_inc(nm_kept, 1)
            dve.sem_inc(zsum_done, 1)
            dve.sem_inc(o_done, 2)
            dve.sem_inc(pt_lo, 2)
            dve.sem_inc(pv_mm, 2)
            nq1 = quads(dve)
            f = pair_fields(dve, 0)
            score(f[0], 0, 0, 0)
            score(f[1], 1, 1, 0)
            with dve.Fori(0, nq1 + 1) as q:
                now = pair_fields(dve, q * 2)
                for k in range(2):
                    ahead = pair_fields(dve, q * 2 + k + 1)
                    for s in range(2):
                        tt = 4 * q + 2 * k + s
                        dve.wait_ge(pt_hi, tt + 1)
                        V.scalar_tensor_tensor(out=pt[s][:, CW:2 * CW], in0=bank[2 + s][:, :], scalar=SP,
                                               in1=pt[s][:, 0:CW], op0=ALU.mult, op1=ALU.subtract).then_inc(pt_lo, 1)
                        score(ahead[s], tt + 2, (2 * k + s + 2) % 4, q + (1 if k else 0))
                        gather(now[s], tt, s)
                    now = ahead

            dve.wait_ge(zsum_done, 4 * nq1 + 5)
            dve.wait_ge(alpha_done, 4 * nq1 + 6)
            dve.wait_ge(o_done, 4 * nq1 + 6)
            step(V.tensor_scalar(z_all[:, 0:T], z_all[:, 0:T], SP * SV, None, ALU.mult))
            step(V.reciprocal(rz[:, :], z_all[:, 0:T]))
            for i in range(T):
                V.scalar_tensor_tensor(out=o_all[:, i, :], in0=o_all[:, i, :], scalar=rz[:, i:i + 1], in1=z[:, i, :],
                                       op0=ALU.mult, op1=ALU.add).then_inc(x2_done, 1)
                if i:
                    dve.wait_ge(x2_done, i)
                    V.bn_stats(bnf[:, i - 1, :], o_all[:, i - 1, :]).then_inc(bnf_done, 1)
                if i > 1:
                    dve.wait_ge(bnf_done, i - 1)
                    V.bn_aggr(mvf[:, i - 2, :], bnf[:, i - 2, :])
            dve.wait_ge(x2_done, T)
            V.bn_stats(bnf[:, T - 1, :], o_all[:, T - 1, :]).then_inc(bnf_done, 1)
            dve.wait_ge(bnf_done, T)
            V.bn_aggr(mvf[:, T - 2, :], bnf[:, T - 2, :])
            V.bn_aggr(mvf[:, T - 1, :], bnf[:, T - 1, :]).then_inc(var_done, 1)
            dve.wait_ge(sdf_done, 1)
            step(V.reciprocal(rstdf[:, :], rstdf[:, :]))
            for i in range(T):
                V.tensor_scalar(o_all[:, i, :], o_all[:, i, :], mvf[:, i, 0:1], rstdf[:, i:i + 1],
                                ALU.subtract, ALU.mult).then_inc(y_done, 1)


def kernel(**inputs):
    import numpy as np
    import concourse.bacc as bacc
    from concourse.bass_utils import run_bass_kernel_spmd

    nc = bacc.Bacc("TRN2", target_bir_lowering=False, num_devices=1)
    host = {k: np.asarray(v) for k, v in inputs.items()}
    layout = {
        "x": host["x"],
        "xT": host["x"].T,
        "adj": host["adj"],
        "adjT": host["adj"].T,
        "t": host["L0_gnn_t"],
        "W": host["L0_gnn_weight"],
        "ptr": host["L1_gnn_ptr"],
        "Wq": host["L1_gnn_Wq"],
        "bq": host["L1_gnn_bq"],
        "Wk": host["L1_gnn_Wk"],
        "bk": host["L1_gnn_bk"],
        "WvT": host["L1_gnn_Wv"].T,
        "bv": host["L1_gnn_bv"],
    }
    arrays, args = {}, []
    for name, a in layout.items():
        a = np.ascontiguousarray(a)
        arrays[f"in_{name}"] = a
        args.append(nc.dram_tensor(f"in_{name}", a.shape, mybir.dt.from_np(a.dtype), kind="ExternalInput").ap())
    shape = host["x"].shape
    out = nc.dram_tensor("out_y", shape, F32, kind="ExternalOutput").ap()
    build(nc, *args, out)
    r = run_bass_kernel_spmd(nc, [arrays], core_ids=[0])
    return r.results[0]["out_y"]
```

```python
from contextlib import ExitStack

import concourse.bass as bass
from concourse import mybir

F32 = mybir.dt.float32
F16 = mybir.dt.float16
BF16 = mybir.dt.bfloat16
I32 = mybir.dt.int32
ALU = mybir.AluOpType
ACT = mybir.ActivationFunctionType
AX = mybir.AxisListType

SP_E, PE_E, DVE_E = mybir.EngineType.SP, mybir.EngineType.PE, mybir.EngineType.DVE

P = 128
EPS = 1e-5
BIG = 1e30
SA = 256.0
SS = 64.0
SZ = 64.0
SW = 1024.0
SK = 64.0
SQ = 256.0
SP = 1024.0
SV = 64.0


def build(nc, x, xT, adj, adjT, t, W, ptr, Wq, bq, Wk, bk, WvT, bv, out):
    N, D = x.shape
    NG = ptr.shape[0]
    T = N // P
    H = D // P
    CW = 512
    NCH = N // CW
    TG = CW // P
    RING = 4
    JB = 2
    NBLK = NCH * T // JB
    UW = N * T // NBLK
    QG = T // JB // RING
    U = N // UW
    assert U == RING and NBLK == T * U
    SMALL = 10
    MAXT = T * NCH
    NT = 3
    KS = SQ * SZ

    with ExitStack() as ctx:
        def sb(name, shape, dt):
            return ctx.enter_context(nc.sbuf_tensor(name, shape, dt))

        def sem(name):
            return ctx.enter_context(nc.semaphore(name))

        z = sb("z", [P, T, D], F32)
        zt_buf = sb("zt_buf", [P, H * 2 * N], F16)
        v_buf = sb("v_buf", [P, T * 2 * D], F16)
        s_buf = sb("s_buf", [P, (T + 1) * 2 * D], F16)
        io_buf = sb("io_buf", [P, (T + 1) * D], F32)
        w_buf = sb("w_buf", [P, RING * JB * CW + UW // 2], F32)
        gid_row = sb("gid_row", [P, N], BF16)
        zt = zt_buf[:, :].rearrange("p (k h n) -> p k h n", k=H, h=2)
        v_hl = v_buf[:, :].rearrange("p (t h d) -> p t h d", t=T, h=2)
        s_hl = s_buf[:, 0:T * 2 * D].rearrange("p (t h d) -> p t h d", t=T, h=2)
        q_hl = s_buf[:, :].rearrange("p (t k h i) -> p t k h i", t=T + 1, k=H, h=2)
        o_all = io_buf[:, :].rearrange("p (t d) -> p t d", d=D)
        x_t = v_buf[:, :].bitcast(F32).rearrange("p (k n) -> p k n", k=H)
        iota_row = zt_buf[:, 0:2 * N].bitcast(F32)
        at_or_after = zt_buf[:, 2 * N:3 * N].bitcast(BF16)
        wtmp = zt_buf[:, 3 * N:4 * N].bitcast(F32)
        wq = wtmp[:, 0:H * D].rearrange("p (k d) -> p k d", k=H)
        wk = wtmp[:, H * D:2 * H * D].rearrange("p (k d) -> p k d", k=H)
        wv = wtmp[:, 2 * H * D:3 * H * D].rearrange("p (k d) -> p k d", k=H)
        raw = [io_buf[:, s * JB * CW:(s + 1) * JB * CW].rearrange("p (j c) -> p j c", j=JB) for s in range(RING)]
        rows = [io_buf[:, RING * JB * CW + s * UW:RING * JB * CW + (s + 1) * UW] for s in range(RING)]
        ahl = [w_buf[:, s * JB * CW:(s + 1) * JB * CW].bitcast(F16).rearrange("p (h j c) -> p h j c", h=2, j=JB)
               for s in range(RING)]
        adjc = [w_buf[:, s * CW:(s + 1) * CW] for s in range(4)]
        prob = [w_buf[:, (4 + s) * CW:(5 + s) * CW] for s in range(2)]
        pt = [w_buf[:, (6 + s) * CW:(7 + s) * CW].bitcast(F16) for s in range(2)]
        pen1 = w_buf[:, 8 * CW:8 * CW + CW // 2].bitcast(BF16)
        def q_raw(u, f):
            return w_buf[:, bass.ds((4 + f) * CW + (u & 1) * (2 * CW), CW)]
        wsb = w_buf[:, 0:H * D].rearrange("p (k d) -> p k d", k=H)
        ident = sb("ident", [P, P], F32)
        ones_bf = sb("ones_bf", [P, P], BF16)
        ones_f = sb("ones_f", [P, P], F32)
        zeros_h = s_buf[:, T * 2 * D:(T + 1) * 2 * D]
        g_hl = sb("g_hl", [P, H, 2, D], F16)
        wv_hl = sb("wv_hl", [P, H, 2, D + 1], F16)
        bv_row = sb("bv_row", [P, D], F32)
        bq_c = sb("bq_c", [P, H], F32)
        bk_c = sb("bk_c", [P, H], F32)
        bqk_p = sb("bqk_p", [P, H], F32)
        kb16 = sb("kb16", [P, H], F32)
        bqk16 = sb("bqk16", [P, 1], F32)
        ptr_i = sb("ptr_i", [P, 1], I32)
        ptr_f = sb("ptr_f", [P, 1], F32)
        tcol = sb("tcol", [P, 1], F32)
        omt = sb("omt", [P, 1], F32)
        tsc0 = sb("tsc0", [P, 1], F32)
        eps_c = sb("eps_c", [P, 1], F32)
        gid_col = sb("gid_col", [P, T + 1], F32)
        nm_q = sb("nm_q", [P, NBLK], F32)
        z_q = sb("z_q", [P, NBLK], F32)
        nm_all = sb("nm_all", [P, T + 1], F32)
        z_all = sb("z_all", [P, T + 1], F32)
        c_all = sb("c_all", [P, T], F32)
        mn0 = sb("mn0", [P, 2], F32)
        stage = sb("stage", [P, TG, D], F32)
        split_f = sb("split_f", [P, 2 * CW], F32)
        bn6 = sb("bn6", [P, TG, 6], F32)
        mv = sb("mv", [P, TG, 2], F32)
        sd = sb("sd", [P, TG], F32)
        rstd = sb("rstd", [P, TG], F32)
        shift = sb("shift", [P, TG], F32)
        pre = sb("pre", [P, 2], F32)
        nnew = sb("nnew", [P, 2], F32)
        pair_buf = sb("pair_buf", [P, 2 * (MAXT + 9)], F32)
        alpha = pair_buf[:, 0:MAXT + 9]
        rsum = pair_buf[:, MAXT + 9:2 * (MAXT + 9)]
        pen0 = [w_buf[:, RING * JB * CW:RING * JB * CW + UW // 2].bitcast(BF16),
                pair_buf[:, 0:UW // 2].bitcast(BF16)]
        mvf = sb("mvf", [P, T, 2], F32)
        bnf = alpha[:, 0:6 * T].rearrange("p (t s) -> p t s", t=T)
        rstdf = sb("rstdf", [P, T], F32)
        shiftf = rsum[:, 0:T]
        rz = sb("rz", [P, T], F32)
        tri = stage[:, :, :].rearrange("p g d -> p (g d)").rearrange("p (i j) -> p i j", i=T)
        clo, chi, cnt, ddif, ge = (split_f[:, CW + i * T:CW + (i + 1) * T] for i in range(5))
        incl = sb("incl", [P, T], F32)
        dif = sb("dif", [P, T + 1], F32)
        tid = sb("tid", [P, NT], F32)
        code = sb("code", [P, NT], F32)
        tmp1 = sb("tmp1", [P, NT], F32)
        NTAB = MAXT + 16
        srow = stage[0:1, :, :].rearrange("p g d -> p (g d)")
        crow = srow[:, 0:NT * P]
        tab_pe = srow[:, NT * P:NT * P + NTAB].bitcast(I32)
        tab_dve = srow[:, NT * P + NTAB:NT * P + 2 * NTAB].bitcast(I32)
        npairs = srow[:, NT * P + 2 * NTAB:NT * P + 2 * NTAB + 1].bitcast(I32)

        bank = [ctx.enter_context(nc.psum_tensor(f"bank{i}", [P, CW], F32)) for i in range(8)]

        small_in = sem("small_in")
        w_in = sem("w_in")
        xt_in = [sem(f"xt_in{i}") for i in range(8)]
        x_in = [sem(f"x_in{i}") for i in range(4)]
        const_done = sem("const_done")
        raw_in = [sem(f"raw_in{s}") for s in range(RING)]
        row_in = [sem(f"row_in{s}") for s in range(RING)]
        setup_v = sem("setup_v")
        cmp_done = sem("cmp_done")
        gid_mm = sem("gid_mm")
        gid_cp = sem("gid_cp")
        gcol_mm = sem("gcol_mm")
        bias_mm = sem("bias_mm")
        g_mm = sem("g_mm")
        weights_done = sem("weights_done")
        s_mm = sem("s_mm")
        s_hi = sem("s_hi")
        s_lo = sem("s_lo")
        s_res = sem("s_res")
        hi_done = sem("hi_done")
        lo_done = sem("lo_done")
        hl_free = sem("hl_free")
        pen_done = sem("pen_done")
        ttr_done = sem("ttr_done")
        min_done = sem("min_done")
        exp_done = sem("exp_done")
        evac = sem("evac")
        bn_done = sem("bn_done")
        mv_done = sem("mv_done")
        sd_done = sem("sd_done")
        rstd_done = sem("rstd_done")
        z_done = sem("z_done")
        z_kept = sem("z_kept")
        zt_mm = sem("zt_mm")
        zt_f = sem("zt_f")
        zt_hi = sem("zt_hi")
        zt_lo = sem("zt_lo")
        v_mm = sem("v_mm")
        v_f = sem("v_f")
        v_hi = sem("v_hi")
        v_lo = sem("v_lo")
        c_done = sem("c_done")
        table_v = sem("table_v")
        code_mm = sem("code_mm")
        table_done = sem("table_done")
        o_zero = sem("o_zero")
        state_v = sem("state_v")
        state_a = sem("state_a")
        q_mm = sem("q_mm")
        q_f = sem("q_f")
        q_split = sem("q_split")
        adj_in = [sem(f"adj_in{s}") for s in range(4)]
        sc_mm = sem("sc_mm")
        sc_read = sem("sc_read")
        pen1_done = sem("pen1_done")
        pre_done = sem("pre_done")
        tsc_done = sem("tsc_done")
        nm_kept = sem("nm_kept")
        prob_done = sem("prob_done")
        alpha_done = sem("alpha_done")
        tr_mm = sem("tr_mm")
        pt_hi = sem("pt_hi")
        pt_lo = sem("pt_lo")
        pv_mm = sem("pv_mm")
        zsum_done = sem("zsum_done")
        o_done = sem("o_done")
        fin_v = sem("fin_v")
        x2_done = sem("x2_done")
        bnf_done = sem("bnf_done")
        var_done = sem("var_done")
        sdf_done = sem("sdf_done")
        statf_done = sem("statf_done")
        rstdf_done = sem("rstdf_done")
        y_done = sem("y_done")
        stored = sem("stored")
        passed = sem("passed")

        block = ctx.enter_context(nc.Block())

        def wait_apart(eng, *waits):
            for s, v in waits:
                eng.wait_ge(s, v)
            eng.sem_inc(passed, 1)

        def quad_codes(eng, engine, table, q):
            _, v = nc.values_load_multi_w_load_instructions(
                table[0:1, bass.ds(q * 4, 4)], engines=[engine], min_val=0, max_val=(1 << 18) - 1,
                skip_runtime_bounds_check_because="the table holds pairs of codes of 9 bits")
            return v

        def fields(eng, v, shift):
            chunk = (v >> shift) & (NCH - 1)
            tile = nc.s_assert_within((v >> (shift + 3)) & 63, 0, T,
                                      skip_runtime_bounds_check_because="the table counts at most T ends")
            return eng.snap(tile), eng.snap(chunk)

        def quads(eng):
            n = eng.value_load(npairs, min_val=T - 1, max_val=MAXT - 1)
            return eng.snap(n >> 2)

        def groups(group):
            group(0, 0, True, False, False)
            group(1, 1, True, True, False)
            return group

        @block.sync
        def _(sp):
            sp.dma_start(ptr_i[0:NG, :], ptr.rearrange("(p o) -> p o", o=1)).then_inc(small_in, 16)
            sp.dma_start(tcol[:, :], t.partition_broadcast(P)).then_inc(small_in, 16)
            sp.dma_start(bv_row[:, :], bv.partition_broadcast(P)).then_inc(small_in, 16)
            sp.dma_start(bq_c[:, :], bq.rearrange("(k p) -> p k", p=P), allow_slow_non_contiguous=True).then_inc(small_in, 16)
            sp.dma_start(bk_c[:, :], bk.rearrange("(k p) -> p k", p=P), allow_slow_non_contiguous=True).then_inc(small_in, 16)
            sp.dma_start(wsb[:, :, :], W.rearrange("(k p) d -> p k d", p=P)).then_inc(w_in, 16)

            def load_xt(i):
                sp.dma_start(x_t[:, :, i * CW:(i + 1) * CW],
                             xT.rearrange("(k p) n -> p k n", p=P)[:, :, i * CW:(i + 1) * CW]).then_inc(xt_in[i], 16)

            load_xt(0)
            for dst, src in ((wq, Wq), (wk, Wk), (wv, WvT)):
                sp.dma_start(dst[:, :, :], src.rearrange("(k p) d -> p k d", p=P)).then_inc(small_in, 16)
            load_xt(1)
            for i in range(4):
                sp.dma_start(z[:, 8 * i:8 * i + 8, :],
                             x.rearrange("(t p) d -> p t d", p=P)[:, 8 * i:8 * i + 8, :]).then_inc(x_in[i], 16)
                for j in (2 * i + 2, 2 * i + 3):
                    if j < 8:
                        load_xt(j)

            def load_block(q, s):
                jb = (q & (QG - 1)) * RING + s
                sp.dma_start(raw[s], adjT[bass.ds(jb * (JB * P), JB * P), bass.ds(((q >> 2) & (NCH - 1)) * CW, CW)]
                             .rearrange("(j p) c -> p j c", p=P)).then_inc(raw_in[s], 16)

            def load_rows(q, s):
                sp.dma_start(rows[s], adj[bass.ds(q * P, P), s * UW:(s + 1) * UW]).then_inc(row_in[s], 16)

            for s in range(RING):
                load_block(0, s)
                load_rows(0, s)
            with sp.Fori(0, T - 1) as q:
                for s in range(RING):
                    wait_apart(sp, (lo_done, RING * q + s + 1))
                    load_block(q + 1, s)
                    sp.wait_ge(exp_done, RING * q + s + 1)
                    load_rows(q + 1, s)

            sp.wait_ge(table_done, 1)
            sp.wait_ge(hl_free, RING + NBLK)
            nq1 = quads(sp)

            def load_chunk(v, sl):
                tile, chunk = fields(sp, v, 0)
                sp.dma_start(adjc[sl], adj[bass.ds(sp.snap((tile & (T - 1)) * P), P),
                                           bass.ds(sp.snap(chunk * CW), CW)]).then_inc(adj_in[sl], 16)

            v = quad_codes(sp, SP_E, tab_pe, 0)
            for sl in range(4):
                load_chunk(v[sl], sl)
            with sp.Fori(0, nq1) as q:
                v = quad_codes(sp, SP_E, tab_pe, q + 1)
                for sl in range(4):
                    wait_apart(sp, (nm_kept, 4 * q + sl + 1))
                    load_chunk(v[sl], sl)
            v = quad_codes(sp, SP_E, tab_pe, nq1 + 1)
            for sl in range(2):
                wait_apart(sp, (nm_kept, 4 * nq1 + sl + 1))
                load_chunk(v[sl], sl)
            with sp.Fori(0, NCH) as g:
                sp.wait_ge(y_done, TG * (g + 1))
                sp.dma_start(out[bass.ds(g * CW, CW), :].rearrange("(t p) d -> p t d", p=P),
                             o_all[:, bass.ds(g * TG, TG), :]).then_inc(stored, 16)
            sp.wait_ge(stored, 16 * NCH)

        @block.tensor
        def _(pe):
            mm = nc.tensor.matmul
            pe.wait_ge(const_done, 1)
            pe.wait_ge(cmp_done, 1)
            for i in range(NCH):
                if i >= 2:
                    pe.wait_ge(gid_cp, i - 1)
                mm(bank[4 + i % 2][:, :], ones_bf[:, :], at_or_after[:, i * CW:(i + 1) * CW],
                   start=True, stop=True).then_inc(gid_mm, 1)
            for i in range(T):
                last = mm(bank[6][:, i:i + 1], at_or_after[:, i * P:(i + 1) * P], ones_bf[:, 0:1],
                          start=True, stop=True)
            last.then_inc(gcol_mm, 1)
            pe.wait_ge(w_in, 16)
            for i in range(T):
                if i % TG == 0:
                    pe.wait_ge(xt_in[i // TG], 16)
                if i >= 4:
                    pe.wait_ge(s_hi, i - 3)
                    pe.wait_ge(s_lo, i - 3)
                    pe.wait_ge(s_res, i - 3)
                for k in range(H):
                    last = mm(bank[i % 4][:, 0:D], x_t[:, k, i * P:(i + 1) * P], wsb[:, k, :],
                              start=(k == 0), stop=(k == H - 1))
                last.then_inc(s_mm, 1)
                if i == 8:
                    pe.wait_ge(small_in, 16 * 8)
                    pe.wait_ge(setup_v, 2)
                    for f in range(H):
                        for k in range(H):
                            mm(bank[6][:, 64 + f:65 + f], wk[:, k, f * P:(f + 1) * P], bq_c[:, k:k + 1],
                               start=(k == 0), stop=(k == H - 1))
                    for f in range(H):
                        for k in range(H):
                            mm(bank[6][:, 68 + f:69 + f], wq[:, k, f * P:(f + 1) * P], bk_c[:, k:k + 1],
                               start=(k == 0), stop=(k == H - 1))
                    for k in range(H):
                        last = mm(bank[6][:, 72:73], ones_f[:, :], bqk_p[:, k:k + 1],
                                  start=(k == 0), stop=(k == H - 1))
                    last.then_inc(bias_mm, 1)
                    for f in range(H):
                        for k in range(H):
                            last = mm(bank[7][:, f * D:(f + 1) * D], wq[:, k, f * P:(f + 1) * P], wk[:, k, :],
                                      start=(k == 0), stop=(k == H - 1))
                    last.then_inc(g_mm, 1)
            pe.wait_ge(s_lo, T)
            pe.wait_ge(s_res, T)
            pe.sem_inc(hl_free, RING)

            def layer0_quad(g, acc, n):
                for s in range(RING):
                    pe.wait_ge(lo_done, (g * QG + n) * RING + s + 1)
                    for j in range(JB):
                        jt = (n * RING + s) * JB + j
                        for i in range(TG):
                            dst = bank[acc + i // 2][:, (i % 2) * D:(i % 2 + 1) * D]
                            for a, b in ((0, 0), (0, 1), (1, 0)):
                                last = mm(dst, ahl[s][:, a, j, i * P:(i + 1) * P],
                                          s_hl[:, bass.ds(jt, 1), b, :].rearrange("p o d -> p (o d)"),
                                          start=False, stop=False, skip_group_check=True)
                    last.then_inc(hl_free, 1)

            def turn_z(g):
                pe.wait_ge(z_done, TG * (g + 1))
                pe.wait_ge(v_f, TG * g)
                for k in range(H):
                    for i in range(TG):
                        last = nc.tensor.transpose(bank[4 + k][:, i * P:(i + 1) * P],
                                                   stage[:, i, k * P:(k + 1) * P], ident[:, :])
                last.then_inc(zt_mm, 1)

            def project_v(g):
                pe.wait_ge(weights_done, 4)
                pe.wait_ge(zt_lo, H * (g + 1))
                for i in range(TG):
                    n = 0
                    for k in range(H):
                        for a, b in ((0, 0), (0, 1), (1, 0)):
                            last = mm(bank[4 + i][:, 0:D + 1], zt[:, k, a, bass.ds((g * TG + i) * P, P)],
                                      wv_hl[:, k, b, :], start=(n == 0), stop=(n == 3 * H - 1))
                            n += 1
                    last.then_inc(v_mm, 1)

            def group(g, par, main, post1, post2):
                acc = 2 * par
                if main:
                    if isinstance(g, int) and g < 2:
                        pass
                    else:
                        pe.wait_ge(evac, TG * (g - 1))
                    for a in range(2):
                        mm(bank[acc + a][:, :], zeros_h[:, 0:P], zeros_h, start=True, stop=False,
                           skip_group_check=True)
                    layer0_quad(g, acc, 0)
                if post2:
                    project_v(g - 2)
                if main:
                    with pe.Fori(1, QG - 1) as n:
                        layer0_quad(g, acc, n)
                if post1:
                    turn_z(g - 1)
                if main:
                    layer0_quad(g, acc, QG - 1)

            groups(group)
            with pe.Fori(1, NCH // 2) as gp:
                group(gp * 2, 0, True, True, True)
                group(gp * 2 + 1, 1, True, True, True)

            def project_q(u, f):
                pe.wait_ge(q_f, 2 * u + f + 1)
                n = 0
                for k in range(H):
                    for a, b in ((0, 0), (0, 1), (1, 0)):
                        last = mm(bank[f][:, :], g_hl[:, k, a, f * P:(f + 1) * P],
                                  zt[:, k, b, bass.ds(u * CW, CW)], start=(n == 0), stop=(n == 3 * H - 1))
                        n += 1
                last.then_inc(q_mm, 1)

            def projections(first, end):
                with pe.Fori(first, end) as u:
                    for f in range(H):
                        project_q(u, f)

            project_v(NCH - 2)
            pe.wait_ge(evac, TG * (NCH - 1))
            projections(0, 3)
            turn_z(NCH - 1)
            pe.wait_ge(table_v, 1)
            pe.wait_ge(evac, TG * NCH)
            for h in range(NT):
                last = mm(bank[2][0:1, h * P:(h + 1) * P], code[:, h:h + 1], ident[:, :], start=True, stop=True)
            last.then_inc(code_mm, 1)
            projections(3, NCH - 2)
            project_v(NCH - 1)
            projections(NCH - 2, NCH)

            def scores(f, s, tt):
                tile, chunk = f
                if not isinstance(tt, int):
                    pe.wait_ge(sc_read, tt - 1)
                n = 0
                for k in range(H):
                    for a, b in ((0, 0), (0, 1), (1, 0)):
                        last = mm(bank[s][:, :], q_hl[:, bass.ds(tile, 1), k, a, :].rearrange("p o i -> p (o i)"),
                                  zt[:, k, b, bass.ds(chunk * CW, CW)], start=(n == 0), stop=(n == 3 * H - 1))
                        n += 1
                last.then_inc(sc_mm, 1)

            def turn(tt, s):
                for c in range(TG):
                    last = nc.tensor.transpose(bank[2 + s][:, c * P:(c + 1) * P],
                                               prob[s][:, c * P:(c + 1) * P], ident[:, :])
                last.then_inc(tr_mm, 1)

            pe.wait_ge(table_done, 1)
            pe.wait_ge(q_split, 4 * NCH + 8)
            pe.wait_ge(v_lo, T)
            nq1 = quads(pe)
            v = quad_codes(pe, PE_E, tab_pe, 0)
            for s in range(2):
                scores(fields(pe, v[s], 0), s, s)
            pe.wait_ge(prob_done, 1)
            turn(0, 0)
            with pe.Fori(0, nq1 + 1) as q:
                v = quad_codes(pe, PE_E, tab_pe, q)
                for k in range(4):
                    s = k % 2
                    tt = 4 * q + k
                    scores(fields(pe, v[k], 9), s, tt + 2)
                    pe.wait_ge(prob_done, tt + 2)
                    pe.wait_ge(pt_lo, tt + 1)
                    turn(tt + 1, 1 - s)
                    chunk = pe.snap(v[k] & (NCH - 1))
                    pe.wait_ge(pt_lo, tt + 2)
                    pe.wait_ge(o_done, tt + 1)
                    n = 0
                    for c in range(TG):
                        for a, b in ((0, 0), (0, 1), (1, 0)):
                            last = mm(bank[6 + s][:, 0:D], pt[s][:, a * CW + c * P:a * CW + (c + 1) * P],
                                      v_hl[:, bass.ds(chunk * TG + c, 1), b, :].rearrange("p o d -> p (o d)"),
                                      start=(n == 0), stop=(n == 3 * TG - 1))
                            n += 1
                    last.then_inc(pv_mm, 1)

        @block.scalar
        def _(act):
            A = nc.scalar.activation
            for i in range(NCH):
                act.wait_ge(gid_mm, i + 1)
                A(gid_row[:, i * CW:(i + 1) * CW], bank[4 + i % 2][:, :], ACT.Copy).then_inc(gid_cp, 1)
            for i in range(T):
                act.wait_ge(s_res, i + 1)
                A(s_hl[:, i, 0, :], bank[i % 4][:, 0:D], ACT.Copy, scale=SS).then_inc(s_hi, 1)

            def quad(g, n, after=()):
                q = g * QG + n
                for s in range(RING):
                    b = RING * q + s
                    act.wait_ge(raw_in[s], 16 * (q + 1))
                    act.wait_ge(hl_free, b + 1)
                    A(ahl[s][:, 0, :, :], raw[s], ACT.Copy, scale=SA).then_inc(hi_done, 1)
                    if not isinstance(b, int) or b >= 2:
                        sums(b - 2, (s - 2) % RING)
                    for at, step in after:
                        if at == s:
                            step()

            def sums(b, s):
                act.wait_ge(min_done, b + 1)
                A(rows[s], rows[s], ACT.Exp, bias=nm_q[:, bass.ds(b, 1)], scale=-1.0,
                  accum_out=z_q[:, bass.ds(b, 1)]).then_inc(exp_done, 1)

            def spread(g):
                act.wait_ge(mv_done, TG * (g + 1))
                A(sd[:, :], mv[:, :, 1], ACT.Sqrt, bias=eps_c[:, :]).then_inc(sd_done, 1)

            def normalise(g, tiles=range(TG)):
                act.wait_ge(rstd_done, 2 * (g + 1))
                for i in tiles:
                    A(stage[:, i, :], stage[:, i, :], ACT.Identity, bias=shift[:, i:i + 1],
                      scale=rstd[:, i:i + 1]).then_inc(z_done, 1)

            def keep_zt(g, halves=range(H)):
                act.wait_ge(zt_mm, g + 1)
                for k in halves:
                    act.wait_ge(v_lo, TG * g)
                    A(split_f[:, k * CW:(k + 1) * CW], bank[4 + k][:, :], ACT.Copy, scale=SZ).then_inc(zt_f, 1)
                    A(zt[:, k, 0, bass.ds(g * CW, CW)], bank[4 + k][:, :], ACT.Copy, scale=SZ).then_inc(zt_hi, 1)

            def keep_v(g, tiles=range(TG)):
                for i in tiles:
                    act.wait_ge(v_f, TG * g + i + 1)
                    A(v_hl[:, bass.ds(g * TG + i, 1), 0, :].rearrange("p o d -> p (o d)"),
                      split_f[:, i * D:(i + 1) * D], ACT.Copy).then_inc(v_hi, 1)

            def group(g, par, main, post1, post2):
                quad(g, 0)
                quad(g, 1, [(1, lambda: spread(g - 1))] if post1 else [])
                steps2, steps3 = [], []
                if post1:
                    steps2 += [(1, lambda: normalise(g - 1, (0, 1))), (2, lambda: normalise(g - 1, (2, 3)))]
                    steps3 += [(2, lambda: keep_zt(g - 1, (0,))), (3, lambda: keep_zt(g - 1, (1,)))]
                if post2:
                    steps2 += [(3, lambda: keep_v(g - 2, (0, 1)))]
                    steps3 += [(0, lambda: keep_v(g - 2, (2, 3)))]
                quad(g, 2, steps2)
                quad(g, 3, steps3)

            groups(group)
            with act.Fori(1, NCH // 2) as gp:
                group(gp * 2, 0, True, True, True)
                group(gp * 2 + 1, 1, True, True, True)
            sums(NBLK - 2, RING - 2)
            sums(NBLK - 1, RING - 1)
            keep_v(NCH - 2)
            spread(NCH - 1)
            normalise(NCH - 1)

            def keep_q(first, end):
                with act.Fori(first, end) as u:
                    for f in range(H):
                        act.wait_ge(q_mm, 2 * u + f + 1)
                        act.wait_ge(q_split, 4 * u + 2 * f + 2)
                        A(q_raw(u, f), bank[f][:, :], ACT.Identity, bias=kb16[:, f:f + 1],
                          scale=SQ / 16 / (SW * SZ)).then_inc(q_f, 1)

            act.sem_inc(q_f, 2)
            keep_q(0, 3)
            keep_zt(NCH - 1)
            act.wait_ge(state_v, 2)
            A(nm_q[:, :], nm_q[:, :], ACT.Exp).then_inc(state_a, 1)
            keep_q(3, NCH - 2)
            keep_v(NCH - 1)
            keep_q(NCH - 2, NCH)

            def soften(tt, s):
                act.wait_ge(tsc_done, tt + 1)
                A(prob[s], prob[s], ACT.Exp, bias=nnew[:, s:s + 1], scale=-1.0,
                  accum_out=rsum[:, bass.ds(tt + 1, 1)]).then_inc(prob_done, 1)
                A(alpha[:, bass.ds(tt + 1, 1)], pre[:, s:s + 1], ACT.Exp, bias=nnew[:, s:s + 1],
                  scale=-1.0).then_inc(alpha_done, 1)

            def high(tt, s):
                act.wait_ge(tr_mm, tt + 1)
                if not isinstance(tt, int):
                    act.wait_ge(pv_mm, tt)
                A(pt[s][:, 0:CW], bank[2 + s][:, :], ACT.Copy, scale=SP).then_inc(pt_hi, 1)

            act.wait_ge(table_done, 1)
            nq1 = quads(act)
            soften(0, 0)
            high(0, 0)
            with act.Fori(0, nq1 + 1) as q:
                for k in range(4):
                    tt = 4 * q + k
                    soften(tt + 1, (k + 1) % 2)
                    high(tt + 1, (k + 1) % 2)

            for g in range(NCH):
                now = slice(g * TG, (g + 1) * TG)
                act.wait_ge(var_done, g + 1)
                A(rstdf[:, now], mvf[:, now, 1], ACT.Sqrt, bias=eps_c[:, :]).then_inc(sdf_done, 1)
                act.wait_ge(statf_done, 2 * (g + 1))
                for i in range(g * TG, (g + 1) * TG):
                    A(o_all[:, i, :], o_all[:, i, :], ACT.Identity, bias=shiftf[:, i:i + 1],
                      scale=rstdf[:, i:i + 1]).then_inc(y_done, 1)

        @block.gpsimd
        def _(pool):
            nc.gpsimd.iota(iota_row, [[1, N]], base=0, channel_multiplier=0,
                           allow_small_or_imprecise_dtypes=True).then_inc(const_done, 1)
            nc.gpsimd.memset(ident[:, :], 0.0).then_inc(const_done, 1)
            pool.wait_ge(const_done, 2)
            nc.gpsimd.affine_select(out=ident[:, :], in_=ident[:, :], compare_op=ALU.not_equal, fill=1.0, base=0,
                                    pattern=[[-1, P]], channel_multiplier=1).then_inc(const_done, 1)
            nc.gpsimd.memset(zeros_h, 0.0).then_inc(const_done, 1)
            nc.gpsimd.memset(tri[:, :, :], 1.0).then_inc(const_done, 1)
            pool.wait_ge(const_done, 5)
            nc.gpsimd.affine_select(out=tri[:, :, :], in_=tri[:, :, :], compare_op=ALU.is_ge, fill=0.0, base=0,
                                    pattern=[[1, T], [-1, T]], channel_multiplier=0).then_inc(const_done, 1)
            nc.gpsimd.iota(tid[:, :], [[P, NT]], base=0, channel_multiplier=1,
                           allow_small_or_imprecise_dtypes=True).then_inc(const_done, 1)

            def keep_z(g):
                pool.wait_ge(z_done, TG * (g + 1))
                nc.gpsimd.tensor_copy(z[:, bass.ds(g * TG, TG), :], stage[:, :, :]).then_inc(z_kept, 1)

            def zt_low(g):
                for k in range(H):
                    pool.wait_ge(zt_hi, H * g + k + 1)
                    nc.gpsimd.tensor_tensor(zt[:, k, 1, bass.ds(g * CW, CW)], split_f[:, k * CW:(k + 1) * CW],
                                            zt[:, k, 0, bass.ds(g * CW, CW)], ALU.subtract).then_inc(zt_lo, 1)

            def v_low(g):
                for i in range(TG):
                    pool.wait_ge(v_hi, TG * g + i + 1)
                    nc.gpsimd.tensor_tensor(v_hl[:, bass.ds(g * TG + i, 1), 1, :].rearrange("p o d -> p (o d)"),
                                            split_f[:, i * D:(i + 1) * D],
                                            v_hl[:, bass.ds(g * TG + i, 1), 0, :].rearrange("p o d -> p (o d)"),
                                            ALU.subtract).then_inc(v_lo, 1)

            keep_z(0)
            zt_low(0)
            with pool.Fori(1, NCH) as g:
                keep_z(g)
                v_low(g - 1)
                zt_low(g)
            v_low(NCH - 1)
            pool.wait_ge(exp_done, NBLK)
            pool.wait_ge(lo_done, NBLK)
            nc.gpsimd.memset(o_all[:, :, :], 0.0).then_inc(o_zero, 1)

        @block.vector
        def _(dve):
            V = nc.vector
            chain = [0]

            def step(ins):
                chain[0] += 1
                ins.then_inc(fin_v, 1)
                dve.wait_ge(fin_v, chain[0])

            V.memset(ones_bf[:, :], 1.0)
            V.memset(ones_f[:, :], 1.0)
            V.memset(eps_c[:, :], EPS)
            V.memset(gid_col[:, T:T + 1], -1.0)
            V.memset(z_all[:, T:T + 1], 0.0)
            V.memset(nm_all[:, T:T + 1], 0.0)
            V.memset(ddif[:, T - 1:T], 0.0)
            step(V.memset(ptr_f[:, :], 1e9))
            dve.wait_ge(small_in, 16 * 8)
            step(V.tensor_copy(ptr_f[0:NG, :], ptr_i[0:NG, :]))
            dve.wait_ge(const_done, 7)
            V.tensor_scalar(at_or_after, iota_row, ptr_f[:, 0:1], None, ALU.is_ge).then_inc(cmp_done, 1)
            step(V.tensor_scalar(omt[:, :], tcol[:, :], -1.0, 1.0, ALU.mult, ALU.add))
            step(V.tensor_scalar(tsc0[:, :], tcol[:, :], 1.0 / (SA * SS), None, ALU.mult))
            V.tensor_tensor(bqk_p[:, :], bq_c[:, :], bk_c[:, :], ALU.mult).then_inc(setup_v, 1)
            step(V.tensor_scalar(bv_row[:, :], bv_row[:, :], SV, None, ALU.mult))
            dve.wait_ge(gcol_mm, 1)
            V.tensor_copy(gid_col[:, 0:T], bank[6][:, 0:T]).then_inc(setup_v, 1)

            def residual(i):
                dve.wait_ge(s_mm, i + 1)
                if i % 8 == 0:
                    dve.wait_ge(x_in[i // 8], 16)
                V.scalar_tensor_tensor(out=z[:, i, :], in0=bank[i % 4][:, 0:D], scalar=omt[:, 0:1],
                                       in1=z[:, i, :], op0=ALU.mult, op1=ALU.add).then_inc(s_res, 1)

            def low(i):
                dve.wait_ge(s_hi, i + 1)
                V.scalar_tensor_tensor(out=s_hl[:, i, 1, :], in0=bank[i % 4][:, 0:D], scalar=SS,
                                       in1=s_hl[:, i, 0, :], op0=ALU.mult, op1=ALU.subtract).then_inc(s_lo, 1)

            for i in range(T):
                residual(i)
                if i:
                    low(i - 1)
            low(T - 1)
            dve.wait_ge(bias_mm, 1)
            dve.wait_ge(g_mm, 1)
            step(V.tensor_scalar(kb16[:, :], bank[6][:, 64:64 + H], SQ / 16, None, ALU.mult))
            step(V.tensor_scalar(bqk16[:, :], bank[6][:, 72:73], 1.0 / 16, None, ALU.mult))
            step(V.tensor_scalar(wv_hl[:, :, 0, 0:D], wv[:, :, :], SW, None, ALU.mult))
            V.scalar_tensor_tensor(out=wv_hl[:, :, 1, 0:D], in0=wv[:, :, :], scalar=SW, in1=wv_hl[:, :, 0, 0:D],
                                   op0=ALU.mult, op1=ALU.subtract).then_inc(weights_done, 1)
            for k in range(H):
                step(V.tensor_scalar(wv_hl[:, k, 0, D:D + 1], bank[6][:, 68 + k:69 + k], SK, None, ALU.mult))
                V.scalar_tensor_tensor(out=wv_hl[:, k, 1, D:D + 1], in0=bank[6][:, 68 + k:69 + k], scalar=SK,
                                       in1=wv_hl[:, k, 0, D:D + 1], op0=ALU.mult,
                                       op1=ALU.subtract).then_inc(weights_done, 1)
            gps = bank[7][:, :].rearrange("p (k d) -> p k d", k=H)
            step(V.tensor_scalar(g_hl[:, :, 0, :], gps, SW, None, ALU.mult))
            V.scalar_tensor_tensor(out=g_hl[:, :, 1, :], in0=gps, scalar=SW, in1=g_hl[:, :, 0, :],
                                   op0=ALU.mult, op1=ALU.subtract).then_inc(weights_done, 1)

            def quad(g, n):
                q = g * QG + n
                for s in range(RING):
                    b = RING * q + s
                    if not isinstance(b, int) or b >= 2:
                        dve.wait_ge(ttr_done, b - 1)
                    V.tensor_scalar(pen0[s % 2], gid_row[:, s * UW:(s + 1) * UW], gid_col[:, bass.ds(q, 1)], BIG,
                                    ALU.is_equal, ALU.mult).then_inc(pen_done, 1)
                    dve.wait_ge(hi_done, b + 1)
                    V.scalar_tensor_tensor(out=ahl[s][:, 1, :, :], in0=raw[s], scalar=SA, in1=ahl[s][:, 0, :, :],
                                           op0=ALU.mult, op1=ALU.subtract).then_inc(lo_done, 1)
                    if not isinstance(b, int) or b >= 1:
                        dve.wait_ge(ttr_done, b)
                        keep_min(b - 1, (s - 1) % 2)
                    wait_apart(dve, (pen_done, b + 1), (row_in[s], 16 * (q + 1)))
                    V.tensor_tensor_reduce(rows[s], rows[s], pen0[s % 2], 2e6, 3e38, ALU.add, ALU.min,
                                           mn0[:, s % 2:s % 2 + 1]).then_inc(ttr_done, 1)

            def keep_min(b, m):
                V.tensor_scalar(nm_q[:, bass.ds(b, 1)], mn0[:, m:m + 1], 1.0, None, ALU.mult).then_inc(min_done, 1)

            def take(g, par):
                dve.wait_ge(hl_free, RING + (g + 1) * QG * RING)
                dve.wait_ge(zt_mm, g)
                dve.wait_ge(z_kept, g)
                for i in range(TG):
                    V.scalar_tensor_tensor(out=stage[:, i, :], in0=bank[2 * par + i // 2][:, (i % 2) * D:(i % 2 + 1) * D],
                                           scalar=tsc0[:, 0:1],
                                           in1=z[:, bass.ds(g * TG + i, 1), :].rearrange("p o d -> p (o d)"),
                                           op0=ALU.mult, op1=ALU.add).then_inc(evac, 1)
                for i in range(TG):
                    dve.wait_ge(evac, TG * g + i + 1)
                    V.bn_stats(bn6[:, i, :], stage[:, i, :]).then_inc(bn_done, 1)
                for i in range(TG):
                    wait_apart(dve, (bn_done, TG * g + i + 1))
                    V.bn_aggr(mv[:, i, :], bn6[:, i, :]).then_inc(mv_done, 1)

            def prepare(g):
                dve.wait_ge(sd_done, g + 1)
                V.reciprocal(rstd[:, :], sd[:, :]).then_inc(rstd_done, 1)
                dve.wait_ge(rstd_done, 2 * g + 1)
                V.scalar_tensor_tensor(out=shift[:, :], in0=mv[:, :, 0], scalar=-1.0, in1=rstd[:, :],
                                       op0=ALU.mult, op1=ALU.mult).then_inc(rstd_done, 1)

            def take_v(g):
                dve.wait_ge(zt_lo, H * (g + 1))
                for i in range(TG):
                    dve.wait_ge(v_mm, TG * g + i + 1)
                    V.tensor_scalar(c_all[:, bass.ds(g * TG + i, 1)], bank[4 + i][:, D:D + 1],
                                    1.0 / (SZ * SK * 16), bqk16[:, 0:1], ALU.mult, ALU.add).then_inc(c_done, 1)
                    V.scalar_tensor_tensor(out=split_f[:, i * D:(i + 1) * D], in0=bank[4 + i][:, 0:D],
                                           scalar=SV / (SZ * SW), in1=bv_row[:, :], op0=ALU.mult,
                                           op1=ALU.add).then_inc(v_f, 1)

            def group(g, par, main, post1, post2):
                if main:
                    quad(g, 0)
                if post1:
                    take(g - 1, 1 - par)
                quad(g, 1)
                if post1:
                    prepare(g - 1)
                if post2:
                    take_v(g - 2)
                quad(g, 2)
                quad(g, 3)

            group(0, 0, True, False, False)
            first = gid_row[:, :].rearrange("p (t i) -> p t i", i=P)[:, :, 0:1].to_broadcast([P, T, NCH])
            last_ = gid_row[:, :].rearrange("p (t i) -> p t i", i=P)[:, :, P - 1:P].to_broadcast([P, T, NCH])
            cfirst = gid_row[:, :].rearrange("p (o c i) -> p o c i", o=1, i=CW)[:, :, :, 0].to_broadcast([P, T, NCH])
            clast = gid_row[:, :].rearrange("p (o c i) -> p o c i", o=1, i=CW)[:, :, :, CW - 1].to_broadcast([P, T, NCH])
            cmp = split_f[:, 0:T * NCH].rearrange("p (t c) -> p t c", t=T)
            step(V.tensor_tensor(cmp, clast, first, ALU.is_lt))
            step(V.tensor_reduce(clo, cmp, AX.X, ALU.add))
            step(V.tensor_tensor(cmp, cfirst, last_, ALU.is_le))
            step(V.tensor_reduce(chi, cmp, AX.X, ALU.add))
            step(V.tensor_tensor(cnt, chi, clo, ALU.subtract))
            step(V.tensor_tensor(tri[:, :, :], tri[:, :, :],
                                 cnt.rearrange("p (o t) -> p o t", o=1).to_broadcast([P, T, T]), ALU.mult))
            step(V.tensor_reduce(incl[:, :], tri[:, :, :], AX.X, ALU.add))
            step(V.tensor_tensor(dif[:, 0:T], chi, incl[:, :], ALU.subtract))
            step(V.tensor_tensor(ddif[:, 0:T - 1], dif[:, 1:T], dif[:, 0:T - 1], ALU.subtract))
            for h in range(NT):
                step(V.tensor_scalar(ge, incl[:, :], tid[:, h:h + 1], None, ALU.is_le))
                step(V.tensor_reduce(code[:, h:h + 1], ge, AX.X, ALU.add))
                step(V.tensor_tensor(ge, ge, ddif[:, :], ALU.mult))
                step(V.tensor_reduce(tmp1[:, h:h + 1], ge, AX.X, ALU.add))
            step(V.scalar_tensor_tensor(out=tmp1[:, :], in0=tmp1[:, :], scalar=dif[:, 0:1], in1=tid[:, :],
                                        op0=ALU.add, op1=ALU.add))
            step(V.scalar_tensor_tensor(out=tmp1[:, :], in0=code[:, :], scalar=T - 0.5, in1=tmp1[:, :],
                                        op0=ALU.is_lt, op1=ALU.mult))
            V.scalar_tensor_tensor(out=code[:, :], in0=code[:, :], scalar=8.0, in1=tmp1[:, :],
                                   op0=ALU.mult, op1=ALU.add).then_inc(table_v, 1)

            group(1, 1, True, True, False)
            with dve.Fori(1, NCH // 2) as gp:
                group(gp * 2, 0, True, True, True)
                group(gp * 2 + 1, 1, True, True, True)
            dve.wait_ge(ttr_done, NBLK)
            keep_min(NBLK - 1, 1)
            take(NCH - 1, (NCH - 1) % 2)
            take_v(NCH - 2)
            prepare(NCH - 1)

            def split_q(first, end):
                with dve.Fori(first, end) as u:
                    for f in range(H):
                        dve.wait_ge(q_f, 2 * u + f + 3)
                        buf = q_raw(u, f).rearrange("p (t i) -> p t i", t=TG)
                        hi = q_hl[:, bass.ds(u * TG, TG), f, 0, :]
                        V.tensor_scalar(hi, buf, 1.0, None, ALU.mult).then_inc(q_split, 1)
                        dve.wait_ge(q_split, 4 * u + 2 * f + 9)
                        V.scalar_tensor_tensor(out=q_hl[:, bass.ds(u * TG, TG), f, 1, :], in0=buf, scalar=1.0,
                                               in1=hi, op0=ALU.mult, op1=ALU.subtract).then_inc(q_split, 1)

            dve.sem_inc(q_split, 8)
            split_q(0, 3)
            dve.wait_ge(exp_done, NBLK)
            dve.wait_ge(min_done, NBLK)
            units = nm_q[:, :].rearrange("p (t u) -> p t u", u=U)
            sums = z_q[:, :].rearrange("p (t u) -> p t u", u=U)
            V.tensor_reduce(nm_all[:, 0:T], units, AX.X, ALU.min).then_inc(state_v, 1)
            dve.wait_ge(state_v, 1)
            V.tensor_tensor(units, nm_all[:, 0:T].rearrange("p (t o) -> p t o", o=1).to_broadcast([P, T, U]), units,
                            ALU.subtract).then_inc(state_v, 1)
            dve.wait_ge(code_mm, 1)
            dve.wait_ge(z_kept, NCH)
            step(V.tensor_copy(crow, bank[2][0:1, 0:NT * P]))
            V.scalar_tensor_tensor(out=tab_pe, in0=crow[:, 2:NTAB + 2], scalar=512.0, in1=crow[:, 0:NTAB],
                                   op0=ALU.mult, op1=ALU.add)
            V.scalar_tensor_tensor(out=tab_dve[:, 1:NTAB], in0=crow[:, 3:NTAB + 2], scalar=512.0,
                                   in1=crow[:, 0:NTAB - 1], op0=ALU.mult, op1=ALU.add)
            V.tensor_scalar(tab_dve[:, 0:1], crow[:, 2:3], 512.0, 8.0 * T, ALU.mult, ALU.add)
            step(V.tensor_scalar(npairs, incl[0:1, T - 1:T], -1.0, None, ALU.add))
            dve.sem_inc(table_done, 1)
            split_q(3, NCH - 2)
            dve.wait_ge(state_a, 1)
            step(V.tensor_tensor(z_q[:, :], z_q[:, :], nm_q[:, :], ALU.mult))
            V.tensor_reduce(z_all[:, 0:T], sums, AX.X, ALU.add)
            take_v(NCH - 1)
            step(V.memset(alpha[:, 0:1], 1.0))
            step(V.memset(rsum[:, 0:1], 0.0))
            dve.wait_ge(c_done, T)
            step(V.tensor_tensor(nm_all[:, 0:T], nm_all[:, 0:T], c_all[:, :], ALU.add))
            split_q(NCH - 2, NCH)
            dve.wait_ge(q_split, 4 * NCH + 8)

            def score(f, tt, sl, q):
                tile, chunk = f
                s = sl % 2
                later = not isinstance(tt, int)
                if later:
                    dve.wait_ge(alpha_done, tt - 1)
                if later or tt:
                    dve.wait_ge(nm_kept, tt)
                V.tensor_scalar(pre[:, s:s + 1], nm_all[:, bass.ds(tile, 1)], 1.0, None, ALU.mult).then_inc(pre_done, 1)
                dve.wait_ge(sc_mm, tt + 1)
                dve.wait_ge(adj_in[sl], 16 * (q + 1))
                V.scalar_tensor_tensor(out=adjc[sl], in0=adjc[sl], scalar=-2.0 * KS, in1=bank[s][:, :],
                                       op0=ALU.mult, op1=ALU.subtract).then_inc(sc_read, 1)
                V.tensor_scalar(pen1, gid_row[:, bass.ds(chunk * CW, CW)], gid_col[:, bass.ds(tile, 1)], BIG,
                                ALU.not_equal, ALU.mult).then_inc(pen1_done, 1)
                waits = [(pre_done, tt + 1), (pen1_done, tt + 1), (sc_read, tt + 1)]
                if later:
                    waits.append((tr_mm, tt - 1))
                wait_apart(dve, *waits)
                V.tensor_tensor_reduce(prob[s], adjc[sl], pen1, 1.0 / KS, pre[:, s:s + 1], ALU.add, ALU.min,
                                       nnew[:, s:s + 1]).then_inc(tsc_done, 1)

            def keep_max(tile, tt, s):
                dve.wait_ge(tsc_done, tt + 1)
                V.tensor_scalar(nm_all[:, bass.ds(tile, 1)], nnew[:, s:s + 1], 1.0, None, ALU.mult).then_inc(nm_kept, 1)

            def gather(tile, after, s):
                al = alpha[:, bass.ds(after, 1)]
                dve.wait_ge(zsum_done, after + 1)
                V.scalar_tensor_tensor(out=z_all[:, bass.ds(tile, 1)], in0=z_all[:, bass.ds(tile, 1)], scalar=al,
                                       in1=rsum[:, bass.ds(after, 1)], op0=ALU.mult, op1=ALU.add).then_inc(zsum_done, 1)
                dve.wait_ge(pv_mm, after + 1)
                dve.wait_ge(o_done, after + 1)
                o = o_all[:, bass.ds(tile, 1), :].rearrange("p o d -> p (o d)")
                V.scalar_tensor_tensor(out=o, in0=o, scalar=al, in1=bank[6 + s][:, 0:D],
                                       op0=ALU.mult, op1=ALU.add).then_inc(o_done, 1)

            dve.wait_ge(o_zero, 1)
            dve.wait_ge(c_done, T)
            dve.sem_inc(zsum_done, 1)
            dve.sem_inc(o_done, 1)
            dve.sem_inc(pt_lo, 1)
            dve.sem_inc(pv_mm, 1)
            nq1 = quads(dve)
            v = quad_codes(dve, DVE_E, tab_pe, 0)
            for s in range(2):
                f = fields(dve, v[s], 0)
                score(f, s, s, 0)
                keep_max(f[0], s, s)
            with dve.Fori(0, nq1 + 1) as q:
                v = quad_codes(dve, DVE_E, tab_dve, q)
                for k in range(4):
                    s = k % 2
                    tt = 4 * q + k
                    ahead = fields(dve, v[k], 9)
                    dve.wait_ge(pt_hi, tt + 1)
                    V.scalar_tensor_tensor(out=pt[s][:, CW:2 * CW], in0=bank[2 + s][:, :], scalar=SP,
                                           in1=pt[s][:, 0:CW], op0=ALU.mult, op1=ALU.subtract).then_inc(pt_lo, 1)
                    score(ahead, tt + 2, (k + 2) % 4, q + k // 2)
                    gather(fields(dve, v[k], 0)[0], tt, 1 - s)
                    keep_max(ahead[0], tt + 2, s)
            v = quad_codes(dve, DVE_E, tab_dve, nq1 + 1)
            gather(fields(dve, v[0], 0)[0], 4 * nq1 + 4, 1)

            dve.wait_ge(zsum_done, 4 * nq1 + 6)
            dve.wait_ge(alpha_done, 4 * nq1 + 5)
            dve.wait_ge(o_done, 4 * nq1 + 6)
            step(V.tensor_scalar(z_all[:, 0:T], z_all[:, 0:T], SP * SV, None, ALU.mult))
            step(V.reciprocal(rz[:, :], z_all[:, 0:T]))

            def stats(g):
                now = slice(g * TG, (g + 1) * TG)
                dve.wait_ge(sdf_done, g + 1)
                V.reciprocal(rstdf[:, now], rstdf[:, now]).then_inc(statf_done, 1)
                dve.wait_ge(statf_done, 2 * g + 1)
                V.scalar_tensor_tensor(out=shiftf[:, now], in0=mvf[:, now, 0], scalar=-1.0, in1=rstdf[:, now],
                                       op0=ALU.mult, op1=ALU.mult).then_inc(statf_done, 1)

            for g in range(NCH):
                tiles = range(g * TG, (g + 1) * TG)
                for i in tiles:
                    V.scalar_tensor_tensor(out=o_all[:, i, :], in0=o_all[:, i, :], scalar=rz[:, i:i + 1],
                                           in1=z[:, i, :], op0=ALU.mult, op1=ALU.add).then_inc(x2_done, 1)
                for i in tiles:
                    dve.wait_ge(x2_done, i + 1)
                    V.bn_stats(bnf[:, i, :], o_all[:, i, :]).then_inc(bnf_done, 1)
                for i in tiles:
                    dve.wait_ge(bnf_done, i + 1)
                    last = V.bn_aggr(mvf[:, i, :], bnf[:, i, :])
                last.then_inc(var_done, 1)
                if g:
                    stats(g - 1)
            stats(NCH - 1)


def kernel(**inputs):
    import numpy as np
    import concourse.bacc as bacc
    from concourse.bass_utils import run_bass_kernel_spmd

    nc = bacc.Bacc("TRN2", target_bir_lowering=False, num_devices=1)
    host = {k: np.asarray(v) for k, v in inputs.items()}
    layout = {
        "x": host["x"],
        "xT": host["x"].T,
        "adj": host["adj"],
        "adjT": host["adj"].T,
        "t": host["L0_gnn_t"],
        "W": host["L0_gnn_weight"],
        "ptr": host["L1_gnn_ptr"],
        "Wq": host["L1_gnn_Wq"],
        "bq": host["L1_gnn_bq"],
        "Wk": host["L1_gnn_Wk"],
        "bk": host["L1_gnn_bk"],
        "WvT": host["L1_gnn_Wv"].T,
        "bv": host["L1_gnn_bv"],
    }
    arrays, args = {}, []
    for name, a in layout.items():
        a = np.ascontiguousarray(a)
        arrays[f"in_{name}"] = a
        args.append(nc.dram_tensor(f"in_{name}", a.shape, mybir.dt.from_np(a.dtype), kind="ExternalInput").ap())
    shape = host["x"].shape
    out = nc.dram_tensor("out_y", shape, F32, kind="ExternalOutput").ap()
    build(nc, *args, out)
    r = run_bass_kernel_spmd(nc, [arrays], core_ids=[0])
    return r.results[0]["out_y"]
```

```python
from contextlib import ExitStack

import concourse.bass as bass
from concourse import mybir

F32 = mybir.dt.float32
F16 = mybir.dt.float16
BF16 = mybir.dt.bfloat16
I32 = mybir.dt.int32
ALU = mybir.AluOpType
ACT = mybir.ActivationFunctionType
AX = mybir.AxisListType

SP_E, PE_E, DVE_E, ACT_E = (mybir.EngineType.SP, mybir.EngineType.PE, mybir.EngineType.DVE,
                            mybir.EngineType.Activation)

P = 128
EPS = 1e-5
BIG = 1e30
ROOT = 2.0 ** 50
SA = 256.0
SS = 64.0
SZ = 64.0
SW = 1024.0
SK = 64.0
SQ = 256.0
SP = 1024.0
SV = 64.0


def build(nc, x, xT, adj, adjT, t, W, ptr, Wq, bq, Wk, bk, WvT, bv, out):
    N, D = x.shape
    NG = ptr.shape[0]
    T = N // P
    H = D // P
    CW = 512
    NCH = N // CW
    TG = CW // P
    RING = 4
    JB = 2
    NBLK = NCH * T // JB
    UW = N * T // NBLK
    QG = T // JB // RING
    U = N // UW
    assert U == RING and NBLK == T * U
    MAXT = T * NCH
    NT = 3
    KS = SQ * SZ
    EARLY = 2
    EARLY_AT = 17
    ROUND = 16
    GID0 = 7

    with ExitStack() as ctx:
        def sb(name, shape, dt):
            return ctx.enter_context(nc.sbuf_tensor(name, shape, dt))

        def sem(name):
            return ctx.enter_context(nc.semaphore(name))

        z = sb("z", [P, T, D], F32)
        zt_buf = sb("zt_buf", [P, H * 2 * N], F16)
        DV = D + 2
        v_buf = sb("v_buf", [P, T * 2 * DV], F16)
        s_buf = sb("s_buf", [P, (T + 1) * 2 * D], F16)
        io_buf = sb("io_buf", [P, (T + 1) * (D + 1)], F32)
        w_buf = sb("w_buf", [P, RING * JB * CW + UW // 2], F32)
        gid_row = sb("gid_row", [P, N], BF16)
        zt = zt_buf[:, :].rearrange("p (k h n) -> p k h n", k=H, h=2)
        v_hl = v_buf[:, :].rearrange("p (t h d) -> p t h d", t=T, h=2)
        s_hl = s_buf[:, 0:T * 2 * D].rearrange("p (t h d) -> p t h d", t=T, h=2)
        q_hl = s_buf[:, :].rearrange("p (t k h i) -> p t k h i", t=T + 1, k=H, h=2)
        o_all = io_buf[:, :].rearrange("p (t d) -> p t d", d=D + 1)
        x_t = v_buf[:, 0:T * 2 * D].bitcast(F32).rearrange("p (k n) -> p k n", k=H)
        iota_row = zt_buf[:, 0:2 * N].bitcast(F32)
        at_or_after = zt_buf[:, 2 * N:3 * N].bitcast(BF16)
        wtmp = zt_buf[:, 3 * N:4 * N].bitcast(F32)
        wq = wtmp[:, 0:H * D].rearrange("p (k d) -> p k d", k=H)
        wk = wtmp[:, H * D:2 * H * D].rearrange("p (k d) -> p k d", k=H)
        wv = wtmp[:, 2 * H * D:3 * H * D].rearrange("p (k d) -> p k d", k=H)
        ones_f = wtmp[:, 3 * H * D + D:3 * H * D + D + P]
        bv_f = wtmp[0:1, 3 * H * D:3 * H * D + D]
        raw = [io_buf[:, s * JB * CW:(s + 1) * JB * CW].rearrange("p (j c) -> p j c", j=JB) for s in range(RING)]
        rows = [io_buf[:, RING * JB * CW + s * UW:RING * JB * CW + (s + 1) * UW] for s in range(RING)]
        ahl = [w_buf[:, s * JB * CW:(s + 1) * JB * CW].bitcast(F16).rearrange("p (h j c) -> p h j c", h=2, j=JB)
               for s in range(RING)]
        adjc = [w_buf[:, s * CW:(s + 1) * CW] for s in range(4)]
        prob = [w_buf[:, (4 + s) * CW:(5 + s) * CW] for s in range(2)]
        pt = [w_buf[:, (6 + s) * CW:(7 + s) * CW].bitcast(F16) for s in range(2)]

        def q_raw(u, f, late):
            if late:
                return split_f[:, f * CW:(f + 1) * CW]
            return w_buf[:, bass.ds((4 + f) * CW + (u & 1) * (2 * CW), CW)]
        wsb = w_buf[:, (RING - 1) * JB * CW:(RING - 1) * JB * CW + H * D].rearrange("p (k d) -> p k d", k=H)
        ident = sb("ident", [P, P], F32)
        ones_bf = sb("ones_bf", [P, P], BF16)
        zeros_h = s_buf[:, T * 2 * D:(T + 1) * 2 * D]
        g_hl = sb("g_hl", [P, H, 2, D], F16)
        wv_hl = sb("wv_hl", [P, H, 2, D + 1], F16)
        brow = sb("brow", [1, 2, D + 1], F16)
        sz_row = sb("sz_row", [1, P], F16)
        bq_c = sb("bq_c", [P, H], F32)
        bk_c = sb("bk_c", [P, H], F32)
        bqk_p = sb("bqk_p", [P, H], F32)
        kb16 = sb("kb16", [P, H], F32)
        ptr_i = sb("ptr_i", [P, 1], I32)
        ptr_f = sb("ptr_f", [P, 1], F32)
        tcol = sb("tcol", [P, 1], F32)
        omt = sb("omt", [P, 1], F32)
        tsc0 = sb("tsc0", [P, 1], F32)
        eps_c = sb("eps_c", [P, 1], F32)
        gid_col = sb("gid_col", [P, T + 1], F32)
        gid_neg = sb("gid_neg", [P, T + 1], F32)
        nm_q = sb("nm_q", [P, NBLK], F32)
        z_q = sb("z_q", [P, NBLK], F32)
        nm_all = sb("nm_all", [P, T + 1], F32)
        z_all = sb("z_all", [P, T], F32)
        c_all = sb("c_all", [P, T], F32)
        mn0 = sb("mn0", [P, 2 * RING], F32)
        stage = sb("stage", [P, TG, D], F32)
        split_f = sb("split_f", [P, 2 * CW], F32)
        bn6 = sb("bn6", [P, TG, 6], F32)
        mv = sb("mv", [P, TG, 2], F32)
        sd = sb("sd", [P, TG], F32)
        rstd = sb("rstd", [P, TG], F32)
        shift = sb("shift", [P, TG], F32)
        pre = sb("pre", [P, 2], F32)
        nnew = sb("nnew", [P, 2], F32)
        pair_buf = sb("pair_buf", [P, 2 * (MAXT + 9)], F32)
        alpha = pair_buf[:, 0:MAXT + 9]
        pen1 = [w_buf[:, 8 * CW:8 * CW + CW // 2].bitcast(BF16),
                pair_buf[:, MAXT + 9:MAXT + 9 + CW // 2].bitcast(BF16)]
        pen0 = [w_buf[:, RING * JB * CW:RING * JB * CW + UW // 2].bitcast(BF16),
                pair_buf[:, 0:UW // 2].bitcast(BF16)]
        mvf = sb("mvf", [P, T, 2], F32)
        bnf = alpha[:, 0:6 * T].rearrange("p (t s) -> p t s", t=T)
        rstdf = sb("rstdf", [P, T], F32)
        shiftf = alpha[:, 6 * T:7 * T]
        rz = sb("rz", [P, T], F32)
        clo, chi, ddif = (w_buf[:, CW + i * T:CW + (i + 1) * T] for i in range(3))
        ge = [w_buf[:, CW + (9 + i) * T:CW + (10 + i) * T] for i in range(6)]
        scan = [w_buf[:, CW + (5 + 2 * i) * T:CW + (7 + 2 * i) * T] for i in range(2)]
        incl = sb("incl", [P, T], F32)
        dif = sb("dif", [P, T + 1], F32)
        tid = sb("tid", [P, NT], F32)
        code = sb("code", [P, NT], F32)
        tmp1 = sb("tmp1", [P, NT], F32)
        NTAB = MAXT + 16
        srow = stage[0:1, :, :].rearrange("p g d -> p (g d)")
        crow = srow[:, 0:NT * P]
        tab_pe = srow[:, NT * P:NT * P + NTAB].bitcast(I32)
        tab_dve = srow[:, NT * P + NTAB:NT * P + 2 * NTAB].bitcast(I32)
        npairs = srow[:, NT * P + 2 * NTAB:NT * P + 2 * NTAB + 1].bitcast(I32)

        bank = [ctx.enter_context(nc.psum_tensor(f"bank{i}", [P, CW], F32)) for i in range(8)]

        small_in = sem("small_in")
        ptr_in = sem("ptr_in")
        iota_done = sem("iota_done")
        w_in = sem("w_in")
        xt_in = [sem(f"xt_in{i}") for i in range(8)]
        x_in = [sem(f"x_in{i}") for i in range(8)]
        const_done = sem("const_done")
        raw_in = [sem(f"raw_in{s}") for s in range(RING)]
        row_in = [sem(f"row_in{s}") for s in range(RING)]
        setup_v = sem("setup_v")
        cmp_done = sem("cmp_done")
        gid_mm = sem("gid_mm")
        gid_cp = sem("gid_cp")
        gcol_mm = sem("gcol_mm")
        bias_mm = sem("bias_mm")
        g_mm = sem("g_mm")
        weights_done = sem("weights_done")
        s_mm = sem("s_mm")
        s_hi = sem("s_hi")
        s_lo = sem("s_lo")
        s_res = sem("s_res")
        hi_done = sem("hi_done")
        lo_done = sem("lo_done")
        hl_free = sem("hl_free")
        pen_done = sem("pen_done")
        ttr_done = sem("ttr_done")
        min_done = sem("min_done")
        exp_done = sem("exp_done")
        evac = sem("evac")
        bn_done = sem("bn_done")
        mv_done = sem("mv_done")
        sd_done = sem("sd_done")
        rstd_done = sem("rstd_done")
        z_done = sem("z_done")
        z_kept = sem("z_kept")
        zt_mm = sem("zt_mm")
        zt_f = sem("zt_f")
        zt_hi = sem("zt_hi")
        zt_lo = sem("zt_lo")
        v_mm = sem("v_mm")
        v_f = sem("v_f")
        v_hi = sem("v_hi")
        v_lo = sem("v_lo")
        v_one = sem("v_one")
        c_done = sem("c_done")
        table_v = sem("table_v")
        code_mm = sem("code_mm")
        table_done = sem("table_done")
        o_zero = sem("o_zero")
        o_ready = sem("o_ready")
        state_v = sem("state_v")
        state_a = sem("state_a")
        q_mm = sem("q_mm")
        q_f = sem("q_f")
        q_split = sem("q_split")
        adj_in = [sem(f"adj_in{s}") for s in range(4)]
        sc_mm = sem("sc_mm")
        sc_read = sem("sc_read")
        pen1_done = sem("pen1_done")
        pre_done = sem("pre_done")
        tsc_done = sem("tsc_done")
        nm_kept = sem("nm_kept")
        prob_done = sem("prob_done")
        alpha_done = sem("alpha_done")
        tr_mm = sem("tr_mm")
        pt_hi = sem("pt_hi")
        pt_lo = sem("pt_lo")
        pv_mm = sem("pv_mm")
        o_done = sem("o_done")
        fin_v = sem("fin_v")
        rz_done = sem("rz_done")
        x2_done = sem("x2_done")
        x2_act = sem("x2_act")
        x2_scaled = sem("x2_scaled")
        x2_pool = sem("x2_pool")
        bnf_done = sem("bnf_done")
        var_done = sem("var_done")
        sdf_done = sem("sdf_done")
        statf_done = sem("statf_done")
        y_done = sem("y_done")
        y_last = sem("y_last")
        stored = sem("stored")
        passed = sem("passed")

        block = ctx.enter_context(nc.Block())

        def wait_apart(eng, *waits):
            for s, v in waits:
                eng.wait_ge(s, v)
            eng.sem_inc(passed, 1)

        def codes(eng, engine, table, r):
            _, v = nc.values_load_multi_w_load_instructions(
                table[0:1, bass.ds(r * ROUND, ROUND)], engines=[engine], min_val=0, max_val=(1 << 18) - 1,
                skip_runtime_bounds_check_because="the table holds pairs of codes of 9 bits")
            return v

        def fields(eng, v, shift):
            chunk = (v >> shift) & (NCH - 1)
            tile = nc.s_assert_within((v >> (shift + 3)) & 63, 0, T,
                                      skip_runtime_bounds_check_because="the table counts at most T ends")
            return eng.snap(tile), eng.snap(chunk)

        def rounds(eng):
            n = eng.value_load(npairs, min_val=T - 1, max_val=MAXT - 1)
            return eng.snap(n // ROUND)

        def slots_left(g):
            return range(EARLY if isinstance(g, int) and g == 0 else 0, RING)

        def groups(group):
            group(0, 0, False, False)
            group(1, 1, True, False)
            return group

        @block.sync
        def _(sp):
            sp.dma_start(wsb[:, :, :], W.rearrange("(k p) d -> p k d", p=P)).then_inc(w_in, 16)

            def load_xt(i):
                sp.dma_start(x_t[:, :, i * CW:(i + 1) * CW],
                             xT.rearrange("(k p) n -> p k n", p=P)[:, :, i * CW:(i + 1) * CW]).then_inc(xt_in[i], 16)

            def load_x(i):
                sp.dma_start(z[:, TG * i:TG * (i + 1), :],
                             x.rearrange("(t p) d -> p t d", p=P)[:, TG * i:TG * (i + 1), :]).then_inc(x_in[i], 16)

            load_xt(0)
            sp.dma_start(ptr_i[0:NG, :], ptr.rearrange("(p o) -> p o", o=1)).then_inc(ptr_in, 16)
            sp.dma_start(tcol[:, :], t.partition_broadcast(P)).then_inc(ptr_in, 16)
            load_x(0)
            load_xt(1)
            load_x(1)
            sp.dma_start(bv_f, bv.rearrange("(o d) -> o d", o=1)).then_inc(small_in, 16)
            sp.dma_start(bq_c[:, :], bq.rearrange("(k p) -> p k", p=P), allow_slow_non_contiguous=True).then_inc(small_in, 16)
            sp.dma_start(bk_c[:, :], bk.rearrange("(k p) -> p k", p=P), allow_slow_non_contiguous=True).then_inc(small_in, 16)
            for dst, src in ((wq, Wq), (wk, Wk), (wv, WvT)):
                sp.dma_start(dst[:, :, :], src.rearrange("(k p) d -> p k d", p=P)).then_inc(small_in, 16)
            def load_block(q, s):
                jb = (q & (QG - 1)) * RING + s
                sp.dma_start(raw[s], adjT[bass.ds(jb * (JB * P), JB * P), bass.ds(((q >> 2) & (NCH - 1)) * CW, CW)]
                             .rearrange("(j p) c -> p j c", p=P)).then_inc(raw_in[s], 16)

            def load_rows(q, s):
                sp.dma_start(rows[s], adj[bass.ds(q * P, P), s * UW:(s + 1) * UW]).then_inc(row_in[s], 16)

            for i in range(2, NCH):
                if i == NCH - 2:
                    for s in range(EARLY):
                        load_block(0, s)
                        load_rows(0, s)
                load_xt(i)
                load_x(i)
            for s in range(EARLY, RING):
                load_block(0, s)
                load_rows(0, s)
            with sp.Fori(0, T - 1) as q:
                for s in range(RING):
                    wait_apart(sp, (lo_done, RING * q + s + 1))
                    load_block(q + 1, s)
                    sp.wait_ge(exp_done, RING * q + s + 1)
                    load_rows(q + 1, s)

            sp.wait_ge(table_done, 1)
            sp.wait_ge(hl_free, RING + NBLK)
            nr1 = rounds(sp)

            def load_chunk(v, tt, sl):
                tile, chunk = fields(sp, v, 0)
                if not isinstance(tt, int):
                    wait_apart(sp, (nm_kept, tt - 3))
                sp.dma_start(adjc[sl], adj[bass.ds(sp.snap((tile & (T - 1)) * P), P),
                                           bass.ds(sp.snap(chunk * CW), CW)]).then_inc(adj_in[sl], 16)

            v = codes(sp, SP_E, tab_pe, 0)
            for k in range(4):
                load_chunk(v[k], k, k)
            with sp.Fori(0, nr1) as r:
                v = codes(sp, SP_E, tab_pe, r)
                for k in range(4, ROUND):
                    load_chunk(v[k], ROUND * r + k, k % 4)
                v = codes(sp, SP_E, tab_pe, r + 1)
                for k in range(4):
                    load_chunk(v[k], ROUND * (r + 1) + k, k)
            v = codes(sp, SP_E, tab_pe, nr1)
            for k in range(4, ROUND):
                load_chunk(v[k], ROUND * nr1 + k, k % 4)
            v = codes(sp, SP_E, tab_pe, nr1 + 1)
            for k in range(2):
                load_chunk(v[k], ROUND * (nr1 + 1) + k, k)
            def store(h):
                sp.dma_start(out[bass.ds(h * 2 * P, 2 * P), :].rearrange("(t p) d -> p t d", p=P),
                             o_all[:, bass.ds(h * 2, 2), 0:D]).then_inc(stored, 16)

            with sp.Fori(0, T // 2 - 1) as h:
                sp.wait_ge(y_done, 2 * (h + 1))
                store(h)
            sp.wait_ge(y_last, 2)
            store(T // 2 - 1)
            sp.wait_ge(stored, 16 * (T // 2))

        @block.tensor
        def _(pe):
            mm = nc.tensor.matmul
            pe.wait_ge(w_in, 16)
            for i in range(T):
                if i % TG == 0:
                    pe.wait_ge(xt_in[i // TG], 16)
                if i >= 4:
                    pe.wait_ge(s_hi, i - 3)
                    pe.wait_ge(s_lo, i - 3)
                    pe.wait_ge(s_res, i - 3)
                for k in range(H):
                    last = mm(bank[i % 4][:, 0:D], x_t[:, k, i * P:(i + 1) * P], wsb[:, k, :],
                              start=(k == 0), stop=(k == H - 1))
                last.then_inc(s_mm, 1)
                if GID0 <= i < GID0 + NCH:
                    n = i - GID0
                    pe.wait_ge(cmp_done, 1)
                    if n >= 2:
                        pe.wait_ge(gid_cp, n - 1)
                    mm(bank[4 + n % 2][:, :], ones_bf[:, :], at_or_after[:, n * CW:(n + 1) * CW],
                       start=True, stop=True).then_inc(gid_mm, 1)
                if i == GID0 + NCH:
                    for n in range(T):
                        last = mm(bank[6][:, n:n + 1], at_or_after[:, n * P:(n + 1) * P], ones_bf[:, 0:1],
                                  start=True, stop=True)
                    last.then_inc(gcol_mm, 1)
                if i == GID0 + NCH + 2:
                    pe.wait_ge(small_in, 16 * 6)
                    pe.wait_ge(setup_v, 2)
                    for f in range(H):
                        for k in range(H):
                            mm(bank[6][:, 64 + f:65 + f], wk[:, k, f * P:(f + 1) * P], bq_c[:, k:k + 1],
                               start=(k == 0), stop=(k == H - 1))
                    for f in range(H):
                        for k in range(H):
                            mm(bank[6][:, 68 + f:69 + f], wq[:, k, f * P:(f + 1) * P], bk_c[:, k:k + 1],
                               start=(k == 0), stop=(k == H - 1))
                    for k in range(H):
                        last = mm(bank[6][:, 72:73], ones_f, bqk_p[:, k:k + 1],
                                  start=(k == 0), stop=(k == H - 1))
                    last.then_inc(bias_mm, 1)
                    for f in range(H):
                        for k in range(H):
                            last = mm(bank[7][:, f * D:(f + 1) * D], wq[:, k, f * P:(f + 1) * P], wk[:, k, :],
                                      start=(k == 0), stop=(k == H - 1))
                    last.then_inc(g_mm, 1)
            pe.wait_ge(const_done, 4)
            pe.wait_ge(s_lo, T)
            pe.wait_ge(s_res, T)
            pe.sem_inc(hl_free, RING)

            def layer0_quad(g, acc, n):
                for s in range(RING):
                    pe.wait_ge(lo_done, (g * QG + n) * RING + s + 1)
                    for j in range(JB):
                        jt = (n * RING + s) * JB + j
                        for i in range(TG):
                            dst = bank[acc + i // 2][:, (i % 2) * D:(i % 2 + 1) * D]
                            for a, b in ((0, 0), (0, 1), (1, 0)):
                                last = mm(dst, ahl[s][:, a, j, i * P:(i + 1) * P],
                                          s_hl[:, bass.ds(jt, 1), b, :].rearrange("p o d -> p (o d)"),
                                          start=False, stop=False, skip_group_check=True)
                    last.then_inc(hl_free, 1)

            def turn_z(g):
                pe.wait_ge(z_done, TG * (g + 1))
                pe.wait_ge(c_done, TG * g)
                for k in range(H):
                    for i in range(TG):
                        last = nc.tensor.transpose(bank[4 + k][:, i * P:(i + 1) * P],
                                                   stage[:, i, k * P:(k + 1) * P], ident[:, :])
                last.then_inc(zt_mm, 1)

            def project_v(g):
                pe.wait_ge(weights_done, 6)
                pe.wait_ge(zt_lo, H * (g + 1))
                for i in range(TG):
                    n = 0
                    for k in range(H):
                        for a, b in ((0, 0), (0, 1), (1, 0)):
                            last = mm(bank[4 + i][:, 0:D + 1], zt[:, k, a, bass.ds((g * TG + i) * P, P)],
                                      wv_hl[:, k, b, :], start=(n == 0), stop=False)
                            n += 1
                    for b in range(2):
                        last = mm(bank[4 + i][:, 0:D + 1], sz_row[:, :], brow[:, b, :], start=False, stop=(b == 1))
                    last.then_inc(v_mm, 1)

            def group(g, par, post1, post2):
                acc = 2 * par
                if post2:
                    pe.wait_ge(evac, 2 * (g - 1))
                for a in range(2):
                    mm(bank[acc + a][:, :], zeros_h[:, 0:P], zeros_h, start=True, stop=False,
                       skip_group_check=True)
                layer0_quad(g, acc, 0)
                if post2:
                    project_v(g - 2)
                with pe.Fori(1, QG - 1) as n:
                    layer0_quad(g, acc, n)
                if post1:
                    turn_z(g - 1)
                layer0_quad(g, acc, QG - 1)

            groups(group)
            with pe.Fori(1, NCH // 2) as gp:
                group(gp * 2, 0, True, True)
                group(gp * 2 + 1, 1, True, True)

            def project_q(u, f, first_bank=0):
                pe.wait_ge(q_f, 2 * u + f + 1)
                n = 0
                for k in range(H):
                    for a, b in ((0, 0), (0, 1), (1, 0)):
                        last = mm(bank[first_bank + f][:, :], g_hl[:, k, a, f * P:(f + 1) * P],
                                  zt[:, k, b, bass.ds(u * CW, CW)], start=(n == 0), stop=(n == 3 * H - 1))
                        n += 1
                last.then_inc(q_mm, 1)

            def last_q(u):
                pe.wait_ge(c_done, T)
                for f in range(H):
                    project_q(u, f, 4)

            def projections(first, end):
                with pe.Fori(first, end) as u:
                    for f in range(H):
                        project_q(u, f)

            project_v(NCH - 2)
            pe.sem_inc(q_f, 2)
            pe.wait_ge(evac, 2 * (NCH - 1))
            projections(0, 3)
            turn_z(NCH - 1)
            pe.wait_ge(table_v, 1)
            pe.wait_ge(evac, 2 * NCH)
            for h in range(NT):
                last = mm(bank[2][0:1, h * P:(h + 1) * P], code[:, h:h + 1], ident[:, :], start=True, stop=True)
            last.then_inc(code_mm, 1)
            projections(3, NCH - 2)
            project_v(NCH - 1)
            pe.wait_ge(table_done, 1)
            nr1 = rounds(pe)
            first_codes = codes(pe, PE_E, tab_pe, 0)
            def scores(f, s, tt):
                tile, chunk = f
                if not isinstance(tt, int):
                    pe.wait_ge(sc_read, tt - 1)
                n = 0
                for k in range(H):
                    for a, b in ((0, 0), (0, 1), (1, 0)):
                        last = mm(bank[s][:, :], q_hl[:, bass.ds(tile, 1), k, a, :].rearrange("p o i -> p (o i)"),
                                  zt[:, k, b, bass.ds(chunk * CW, CW)], start=(n == 0), stop=(n == 3 * H - 1))
                        n += 1
                last.then_inc(sc_mm, 1)

            def turn(tt, s):
                for c in range(TG):
                    last = nc.tensor.transpose(bank[2 + s][:, c * P:(c + 1) * P],
                                               prob[s][:, c * P:(c + 1) * P], ident[:, :])
                last.then_inc(tr_mm, 1)

            pe.wait_ge(q_f, 2 * (NCH - 2) + 2)
            pe.wait_ge(q_split, 4 * (NCH - 2) + 8)
            for s in range(2):
                scores(fields(pe, first_codes[s], 0), s, s)
            last_q(NCH - 2)
            last_q(NCH - 1)
            pe.wait_ge(prob_done, 1)
            turn(0, 0)
            with pe.Fori(0, nr1 + 1) as r:
                v = codes(pe, PE_E, tab_pe, r)
                for k in range(ROUND):
                    s = k % 2
                    tt = ROUND * r + k
                    if k == 4:
                        pe.wait_ge(q_split, 4 * NCH + 8)
                    scores(fields(pe, v[k], 9), s, tt + 2)
                    pe.wait_ge(prob_done, tt + 2)
                    pe.wait_ge(pt_lo, tt + 1)
                    turn(tt + 1, 1 - s)
                    chunk = pe.snap(v[k] & (NCH - 1))
                    pe.wait_ge(pt_lo, tt + 2)
                    pe.wait_ge(o_done, tt + 1)
                    if k == 0:
                        pe.wait_ge(v_lo, T)
                        pe.wait_ge(v_one, 2)
                    n = 0
                    for c in range(TG):
                        for a, b in ((0, 0), (0, 1), (1, 0)):
                            last = mm(bank[6 + s][:, 0:D + 1], pt[s][:, a * CW + c * P:a * CW + (c + 1) * P],
                                      v_hl[:, bass.ds(chunk * TG + c, 1), b, 0:D + 1].rearrange("p o d -> p (o d)"),
                                      start=(n == 0), stop=(n == 3 * TG - 1))
                            n += 1
                    last.then_inc(pv_mm, 1)

        @block.scalar
        def _(act):
            A = nc.scalar.activation
            def quad(g, n, after=(), slots=range(RING)):
                q = g * QG + n
                for s in slots:
                    b = RING * q + s
                    act.wait_ge(raw_in[s], 16 * (q + 1))
                    if not isinstance(b, int) or b >= RING - 1:
                        act.wait_ge(hl_free, b + 1)
                    A(ahl[s][:, 0, :, :], raw[s], ACT.Copy, scale=SA).then_inc(hi_done, 1)
                    if not isinstance(b, int) or b >= 2:
                        sums(b - 2, (n * RING + s - 2) % (2 * RING))
                    for at, step in after:
                        if at == s:
                            step()

            def sums(b, m):
                act.wait_ge(ttr_done, b + 1)
                A(rows[m % RING], rows[m % RING], ACT.Exp, bias=mn0[:, m:m + 1], scale=-1.0,
                  accum_out=z_q[:, bass.ds(b, 1)]).then_inc(exp_done, 1)

            def spread(g):
                act.wait_ge(mv_done, TG * (g + 1))
                A(sd[:, :], mv[:, :, 1], ACT.Sqrt, bias=eps_c[:, :]).then_inc(sd_done, 1)

            def normalise(g, tiles=range(TG)):
                act.wait_ge(rstd_done, 2 * (g + 1))
                for i in tiles:
                    A(stage[:, i, :], stage[:, i, :], ACT.Identity, bias=shift[:, i:i + 1],
                      scale=rstd[:, i:i + 1]).then_inc(z_done, 1)

            def keep_zt(g, halves=range(H)):
                act.wait_ge(zt_mm, g + 1)
                for k in halves:
                    act.wait_ge(v_lo, TG * g)
                    A(split_f[:, k * CW:(k + 1) * CW], bank[4 + k][:, :], ACT.Copy, scale=SZ).then_inc(zt_f, 1)
                    A(zt[:, k, 0, bass.ds(g * CW, CW)], bank[4 + k][:, :], ACT.Copy, scale=SZ).then_inc(zt_hi, 1)

            def keep_v(g, tiles=range(TG)):
                act.wait_ge(zt_lo, H * (g + 1))
                for i in tiles:
                    act.wait_ge(v_mm, TG * g + i + 1)
                    A(split_f[:, i * D:(i + 1) * D], bank[4 + i][:, 0:D], ACT.Copy,
                      scale=SV / (SZ * SW)).then_inc(v_f, 1)
                    A(v_hl[:, bass.ds(g * TG + i, 1), 0, 0:D].rearrange("p o d -> p (o d)"),
                      bank[4 + i][:, 0:D], ACT.Copy, scale=SV / (SZ * SW)).then_inc(v_hi, 1)
                    A(c_all[:, bass.ds(g * TG + i, 1)], bank[4 + i][:, D:D + 1], ACT.Copy,
                      scale=1.0 / (SZ * SK * 16)).then_inc(c_done, 1)

            def group(g, par, post1, post2):
                quad(g, 0, slots=slots_left(g))
                steps1, steps2, steps3 = [], [], []
                if post1:
                    steps1 += [(1, lambda: spread(g - 1))]
                    steps2 += [(1, lambda: normalise(g - 1, (0, 1))), (2, lambda: normalise(g - 1, (2, 3)))]
                    steps3 += [(2, lambda: keep_zt(g - 1, (0,))), (3, lambda: keep_zt(g - 1, (1,)))]
                if post2:
                    steps1 += [(3, lambda: keep_v(g - 2, (0, 1)))]
                    steps2 += [(0, lambda: keep_v(g - 2, (2, 3)))]
                quad(g, 1, steps1)
                quad(g, 2, steps2)
                quad(g, 3, steps3)

            for i in range(T):
                act.wait_ge(s_res, i + 1)
                A(s_hl[:, i, 0, :], bank[i % 4][:, 0:D], ACT.Copy, scale=SS).then_inc(s_hi, 1)
                if GID0 <= i < GID0 + NCH:
                    n = i - GID0
                    act.wait_ge(gid_mm, n + 1)
                    A(gid_row[:, n * CW:(n + 1) * CW], bank[4 + n % 2][:, :], ACT.Copy).then_inc(gid_cp, 1)
                if i == EARLY_AT:
                    quad(0, 0, slots=range(EARLY))

            groups(group)
            with act.Fori(1, NCH // 2) as gp:
                group(gp * 2, 0, True, True)
                group(gp * 2 + 1, 1, True, True)
            sums(NBLK - 2, 2 * RING - 2)
            sums(NBLK - 1, 2 * RING - 1)
            def keep_q(u, first_bank=0):
                for f in range(H):
                    act.wait_ge(q_mm, 2 * u + f + 1)
                    act.wait_ge(q_split, 4 * u + f + 3)
                    A(q_raw(u, f, first_bank > 0), bank[first_bank + f][:, :], ACT.Identity, bias=kb16[:, f:f + 1],
                      scale=SQ / 16 / (SW * SZ)).then_inc(q_f, 1)

            def keep_qs(first, end):
                with act.Fori(first, end) as u:
                    keep_q(u)

            keep_qs(0, 1)
            spread(NCH - 1)
            keep_v(NCH - 2, (0, 1, 2))
            keep_qs(1, 2)
            keep_v(NCH - 2, (3,))
            normalise(NCH - 1)
            keep_qs(2, 3)
            keep_zt(NCH - 1)
            act.wait_ge(state_v, 2)
            A(nm_q[:, :], nm_q[:, :], ACT.Exp).then_inc(state_a, 1)
            keep_qs(3, NCH - 2)
            keep_v(NCH - 1)

            def penalty(f, tt, s):
                tile, chunk = f
                if not isinstance(tt, int):
                    act.wait_ge(tsc_done, tt - 1)
                A(pen1[s], gid_row[:, bass.ds(chunk * CW, CW)], ACT.Square, bias=gid_neg[:, bass.ds(tile, 1)],
                  scale=ROOT).then_inc(pen1_done, 1)

            def soften(tt, s):
                act.wait_ge(tsc_done, tt + 1)
                A(prob[s], prob[s], ACT.Exp, bias=nnew[:, s:s + 1], scale=-1.0).then_inc(prob_done, 1)

            def decay(tt, s):
                A(alpha[:, bass.ds(tt + 1, 1)], pre[:, s:s + 1], ACT.Exp, bias=nnew[:, s:s + 1],
                  scale=-1.0).then_inc(alpha_done, 1)

            def high(tt, s):
                act.wait_ge(tr_mm, tt + 1)
                if not isinstance(tt, int):
                    act.wait_ge(pv_mm, tt)
                A(pt[s][:, 0:CW], bank[2 + s][:, :], ACT.Copy, scale=SP).then_inc(pt_hi, 1)

            act.wait_ge(table_done, 1)
            nr1 = rounds(act)
            v = codes(act, ACT_E, tab_pe, 0)
            act.wait_ge(ttr_done, NBLK)
            for s in range(2):
                penalty(fields(act, v[s], 0), s, s)
            act.wait_ge(v_lo, T)
            keep_q(NCH - 2, 4)
            soften(0, 0)
            decay(0, 0)
            act.wait_ge(q_split, 4 * (NCH - 1) + 8)
            keep_q(NCH - 1, 4)
            high(0, 0)
            with act.Fori(0, nr1 + 1) as r:
                v = codes(act, ACT_E, tab_pe, r)
                for k in range(ROUND):
                    s = k % 2
                    tt = ROUND * r + k
                    soften(tt + 1, 1 - s)
                    penalty(fields(act, v[k], 9), tt + 2, s)
                    decay(tt + 1, 1 - s)
                    high(tt + 1, 1 - s)

            act.wait_ge(rz_done, 1)
            for i in range(TG - 2, T, TG):
                A(o_all[:, i, 0:D], o_all[:, i, 0:D], ACT.Copy, scale=rz[:, i:i + 1]).then_inc(x2_act, 1)
            for g in range(NCH):
                now = slice(g * TG, (g + 1) * TG)
                act.wait_ge(var_done, g + 1)
                A(rstdf[:, now], mvf[:, now, 1], ACT.Sqrt, bias=eps_c[:, :]).then_inc(sdf_done, 1)
                act.wait_ge(statf_done, 2 * (g + 1))
                for i in range(g * TG, min((g + 1) * TG, T - 2)):
                    A(o_all[:, i, 0:D], o_all[:, i, 0:D], ACT.Identity, bias=shiftf[:, i:i + 1],
                      scale=rstdf[:, i:i + 1]).then_inc(y_done, 1)

        @block.gpsimd
        def _(pool):
            nc.gpsimd.iota(iota_row, [[1, N]], base=0, channel_multiplier=0,
                           allow_small_or_imprecise_dtypes=True).then_inc(iota_done, 1)
            nc.gpsimd.memset(ident[:, :], 0.0).then_inc(const_done, 1)
            pool.wait_ge(const_done, 1)
            nc.gpsimd.affine_select(out=ident[:, :], in_=ident[:, :], compare_op=ALU.not_equal, fill=1.0, base=0,
                                    pattern=[[-1, P]], channel_multiplier=1).then_inc(const_done, 1)
            nc.gpsimd.memset(zeros_h, 0.0).then_inc(const_done, 1)
            nc.gpsimd.iota(tid[:, :], [[P, NT]], base=0, channel_multiplier=1,
                           allow_small_or_imprecise_dtypes=True).then_inc(const_done, 1)

            def keep_z(g):
                pool.wait_ge(z_done, TG * (g + 1))
                nc.gpsimd.tensor_copy(z[:, bass.ds(g * TG, TG), :], stage[:, :, :]).then_inc(z_kept, 1)

            def zt_low(g):
                for k in range(H):
                    pool.wait_ge(zt_hi, H * g + k + 1)
                    nc.gpsimd.tensor_tensor(zt[:, k, 1, bass.ds(g * CW, CW)], split_f[:, k * CW:(k + 1) * CW],
                                            zt[:, k, 0, bass.ds(g * CW, CW)], ALU.subtract).then_inc(zt_lo, 1)

            def v_low(g):
                for i in range(TG):
                    pool.wait_ge(v_hi, TG * g + i + 1)
                    pool.wait_ge(v_f, TG * g + i + 1)
                    nc.gpsimd.tensor_tensor(v_hl[:, bass.ds(g * TG + i, 1), 1, 0:D].rearrange("p o d -> p (o d)"),
                                            split_f[:, i * D:(i + 1) * D],
                                            v_hl[:, bass.ds(g * TG + i, 1), 0, 0:D].rearrange("p o d -> p (o d)"),
                                            ALU.subtract).then_inc(v_lo, 1)

            pool.wait_ge(hl_free, RING)
            nc.gpsimd.memset(v_hl[:, :, 0, D:DV], SV).then_inc(v_one, 1)
            nc.gpsimd.memset(v_hl[:, :, 1, D:DV], 0.0).then_inc(v_one, 1)
            keep_z(0)
            zt_low(0)
            with pool.Fori(2, NCH) as g:
                v_low(g - 2)
                keep_z(g - 1)
                zt_low(g - 1)
            pool.wait_ge(exp_done, NBLK)
            pool.wait_ge(lo_done, NBLK)
            nc.gpsimd.memset(o_all[:, :, :], 0.0).then_inc(o_zero, 1)
            v_low(NCH - 2)
            keep_z(NCH - 1)
            zt_low(NCH - 1)
            v_low(NCH - 1)
            pool.wait_ge(rz_done, 1)
            for g in range(NCH):
                i = (g + 1) * TG - 2
                pool.wait_ge(x2_act, g + 1)
                nc.gpsimd.tensor_tensor(o_all[:, i, 0:D], o_all[:, i, 0:D], z[:, i, :], ALU.add).then_inc(x2_pool, 1)
                i = (g + 1) * TG - 1
                nc.gpsimd.tensor_scalar(o_all[:, i, 0:D], o_all[:, i, 0:D], rz[:, i:i + 1], None,
                                        ALU.mult).then_inc(x2_scaled, 1)
                pool.wait_ge(x2_scaled, g + 1)
                nc.gpsimd.tensor_tensor(o_all[:, i, 0:D], o_all[:, i, 0:D], z[:, i, :], ALU.add).then_inc(x2_pool, 1)

        @block.vector
        def _(dve):
            V = nc.vector
            chain = [0]

            def step(ins):
                chain[0] += 1
                ins.then_inc(fin_v, 1)
                dve.wait_ge(fin_v, chain[0])

            V.memset(ones_bf[:, :], 1.0)
            V.memset(ones_f, 1.0)
            V.memset(sz_row[:, :], SZ)
            V.memset(eps_c[:, :], EPS)
            V.memset(gid_col[:, T:T + 1], -1.0)
            V.memset(nm_all[:, T:T + 1], 0.0)
            step(V.memset(ptr_f[:, :], 1e9))
            dve.wait_ge(ptr_in, 16 * 2)
            step(V.tensor_copy(ptr_f[0:NG, :], ptr_i[0:NG, :]))
            dve.wait_ge(iota_done, 1)
            V.tensor_scalar(at_or_after, iota_row, ptr_f[:, 0:1], None, ALU.is_ge).then_inc(cmp_done, 1)
            step(V.tensor_scalar(omt[:, :], tcol[:, :], -1.0, 1.0, ALU.mult, ALU.add))
            step(V.tensor_scalar(tsc0[:, :], tcol[:, :], 1.0 / (SA * SS), None, ALU.mult))

            def residual(i):
                dve.wait_ge(s_mm, i + 1)
                if i % TG == 0:
                    dve.wait_ge(x_in[i // TG], 16)
                V.scalar_tensor_tensor(out=z[:, i, :], in0=bank[i % 4][:, 0:D], scalar=omt[:, 0:1],
                                       in1=z[:, i, :], op0=ALU.mult, op1=ALU.add).then_inc(s_res, 1)

            def low(i):
                dve.wait_ge(s_hi, i + 1)
                V.scalar_tensor_tensor(out=s_hl[:, i, 1, :], in0=bank[i % 4][:, 0:D], scalar=SS,
                                       in1=s_hl[:, i, 0, :], op0=ALU.mult, op1=ALU.subtract).then_inc(s_lo, 1)

            def quad(g, n, slots=range(RING)):
                q = g * QG + n
                for s in slots:
                    b = RING * q + s
                    if not isinstance(b, int) or b >= 2:
                        dve.wait_ge(ttr_done, b - 1)
                    V.tensor_scalar(pen0[s % 2], gid_row[:, s * UW:(s + 1) * UW], gid_col[:, bass.ds(q, 1)], BIG,
                                    ALU.is_equal, ALU.mult).then_inc(pen_done, 1)
                    dve.wait_ge(hi_done, b + 1)
                    V.scalar_tensor_tensor(out=ahl[s][:, 1, :, :], in0=raw[s], scalar=SA, in1=ahl[s][:, 0, :, :],
                                           op0=ALU.mult, op1=ALU.subtract).then_inc(lo_done, 1)
                    if s == 0 and (not isinstance(b, int) or b >= 1):
                        keep_min(q - 1, (n - 1) % 2)
                    wait_apart(dve, (pen_done, b + 1), (row_in[s], 16 * (q + 1)))
                    m = (n * RING + s) % (2 * RING)
                    V.tensor_tensor_reduce(rows[s], rows[s], pen0[s % 2], 2e6, 3e38, ALU.add, ALU.min,
                                           mn0[:, m:m + 1]).then_inc(ttr_done, 1)

            def keep_min(q, half):
                dve.wait_ge(ttr_done, RING * (q + 1))
                V.tensor_scalar(nm_q[:, bass.ds(RING * q, RING)], mn0[:, half * RING:(half + 1) * RING],
                                1.0, None, ALU.mult).then_inc(min_done, 1)

            def split_weights():
                dve.wait_ge(bias_mm, 1)
                dve.wait_ge(g_mm, 1)
                step(V.tensor_scalar(kb16[:, :], bank[6][:, 64:64 + H], SQ / 16, None, ALU.mult))
                for part, src, scale in ((brow[:, :, 0:D], bv_f, SW), (brow[:, :, D:D + 1], bank[6][0:1, 72:73], SK)):
                    step(V.tensor_scalar(part[:, 0, :], src, scale, None, ALU.mult))
                    V.scalar_tensor_tensor(out=part[:, 1, :], in0=src, scalar=scale, in1=part[:, 0, :],
                                           op0=ALU.mult, op1=ALU.subtract).then_inc(weights_done, 1)
                step(V.tensor_scalar(wv_hl[:, :, 0, 0:D], wv[:, :, :], SW, None, ALU.mult))
                V.scalar_tensor_tensor(out=wv_hl[:, :, 1, 0:D], in0=wv[:, :, :], scalar=SW, in1=wv_hl[:, :, 0, 0:D],
                                       op0=ALU.mult, op1=ALU.subtract).then_inc(weights_done, 1)
                for k in range(H):
                    step(V.tensor_scalar(wv_hl[:, k, 0, D:D + 1], bank[6][:, 68 + k:69 + k], SK, None, ALU.mult))
                    V.scalar_tensor_tensor(out=wv_hl[:, k, 1, D:D + 1], in0=bank[6][:, 68 + k:69 + k], scalar=SK,
                                           in1=wv_hl[:, k, 0, D:D + 1], op0=ALU.mult,
                                           op1=ALU.subtract).then_inc(weights_done, 1)
                gps = bank[7][:, :].rearrange("p (k d) -> p k d", k=H)
                step(V.tensor_scalar(g_hl[:, :, 0, :], gps, SW, None, ALU.mult))
                V.scalar_tensor_tensor(out=g_hl[:, :, 1, :], in0=gps, scalar=SW, in1=g_hl[:, :, 0, :],
                                       op0=ALU.mult, op1=ALU.subtract).then_inc(weights_done, 1)

            for i in range(T):
                residual(i)
                if i:
                    low(i - 1)
                if i == GID0 + NCH + 1:
                    dve.wait_ge(small_in, 16 * 6)
                    V.tensor_tensor(bqk_p[:, :], bq_c[:, :], bk_c[:, :], ALU.mult).then_inc(setup_v, 1)
                    dve.wait_ge(gcol_mm, 1)
                    V.tensor_copy(gid_col[:, 0:T], bank[6][:, 0:T]).then_inc(setup_v, 1)
                    dve.wait_ge(setup_v, 2)
                    V.tensor_scalar(gid_neg[:, :], gid_col[:, :], -ROOT, None, ALU.mult).then_inc(setup_v, 1)
                if i == EARLY_AT:
                    quad(0, 0, range(EARLY))
            low(T - 1)

            def take(g, par):
                dve.wait_ge(hl_free, RING + (g + 1) * QG * RING)
                dve.wait_ge(zt_mm, g)
                dve.wait_ge(z_kept, g)
                for i in range(2):
                    V.scalar_tensor_tensor(out=stage[:, 2 * i:2 * i + 2, :],
                                           in0=bank[2 * par + i][:, :].rearrange("p (t d) -> p t d", t=2),
                                           scalar=tsc0[:, 0:1], in1=z[:, bass.ds(g * TG + 2 * i, 2), :],
                                           op0=ALU.mult, op1=ALU.add).then_inc(evac, 1)
                for i in range(TG):
                    dve.wait_ge(evac, 2 * g + i // 2 + 1)
                    V.bn_stats(bn6[:, i, :], stage[:, i, :]).then_inc(bn_done, 1)
                for i in range(TG):
                    wait_apart(dve, (bn_done, TG * g + i + 1))
                    V.bn_aggr(mv[:, i, :], bn6[:, i, :]).then_inc(mv_done, 1)

            def prepare(g):
                dve.wait_ge(sd_done, g + 1)
                V.reciprocal(rstd[:, :], sd[:, :]).then_inc(rstd_done, 1)
                dve.wait_ge(rstd_done, 2 * g + 1)
                V.scalar_tensor_tensor(out=shift[:, :], in0=mv[:, :, 0], scalar=-1.0, in1=rstd[:, :],
                                       op0=ALU.mult, op1=ALU.mult).then_inc(rstd_done, 1)

            def group(g, par, post1, post2):
                quad(g, 0, slots_left(g))
                if isinstance(g, int) and g == 0:
                    split_weights()
                if post1:
                    take(g - 1, 1 - par)
                quad(g, 1)
                if post1:
                    prepare(g - 1)
                quad(g, 2)
                quad(g, 3)

            group(0, 0, False, False)
            group(1, 1, True, False)
            with dve.Fori(1, NCH // 2) as gp:
                group(gp * 2, 0, True, True)
                group(gp * 2 + 1, 1, True, True)
            dve.sem_inc(q_split, 8)
            keep_min(T - 1, 1)

            def codes_of_pairs():
                first = gid_row[:, :].rearrange("p (t i) -> p t i", i=P)[:, :, 0:1].to_broadcast([P, T, NCH])
                last_ = gid_row[:, :].rearrange("p (t i) -> p t i", i=P)[:, :, P - 1:P].to_broadcast([P, T, NCH])
                cfirst = gid_row[:, :].rearrange("p (o c i) -> p o c i", o=1, i=CW)[:, :, :, 0].to_broadcast([P, T, NCH])
                clast = gid_row[:, :].rearrange("p (o c i) -> p o c i", o=1, i=CW)[:, :, :, CW - 1].to_broadcast([P, T, NCH])
                cmp = w_buf[:, 0:T * NCH].rearrange("p (t c) -> p t c", t=T)
                dve.wait_ge(const_done, 4)
                V.memset(ddif[:, T - 1:T], 0.0)
                step(V.tensor_tensor(cmp, clast, first, ALU.is_lt))
                step(V.tensor_reduce(clo, cmp, AX.X, ALU.add))
                step(V.tensor_tensor(cmp, cfirst, last_, ALU.is_le))
                step(V.tensor_reduce(chi, cmp, AX.X, ALU.add))
                V.memset(scan[0][:, 0:T], 0.0)
                V.memset(scan[1][:, 0:T], 0.0)
                step(V.tensor_tensor(scan[0][:, T:2 * T], chi, clo, ALU.subtract))
                far, part = 1, 0
                while far < T:
                    dst = incl[:, :] if 2 * far >= T else scan[1 - part][:, T:2 * T]
                    step(V.tensor_tensor(dst, scan[part][:, T:2 * T], scan[part][:, T - far:2 * T - far], ALU.add))
                    far, part = 2 * far, 1 - part
                step(V.tensor_tensor(dif[:, 0:T], chi, incl[:, :], ALU.subtract))
                step(V.tensor_tensor(ddif[:, 0:T - 1], dif[:, 1:T], dif[:, 0:T - 1], ALU.subtract))
                for h in range(NT):
                    V.scalar_tensor_tensor(out=ge[h], in0=incl[:, :], scalar=tid[:, h:h + 1], in1=ones_bf[:, 0:T],
                                           op0=ALU.is_le, op1=ALU.mult, accum_out=code[:, h:h + 1])
                    last = V.scalar_tensor_tensor(out=ge[NT + h], in0=incl[:, :], scalar=tid[:, h:h + 1], in1=ddif,
                                                  op0=ALU.is_le, op1=ALU.mult, accum_out=tmp1[:, h:h + 1])
                step(last)
                step(V.scalar_tensor_tensor(out=tmp1[:, :], in0=tmp1[:, :], scalar=dif[:, 0:1], in1=tid[:, :],
                                            op0=ALU.add, op1=ALU.add))
                step(V.scalar_tensor_tensor(out=tmp1[:, :], in0=code[:, :], scalar=T - 0.5, in1=tmp1[:, :],
                                            op0=ALU.is_lt, op1=ALU.mult))
                V.scalar_tensor_tensor(out=code[:, :], in0=code[:, :], scalar=8.0, in1=tmp1[:, :],
                                       op0=ALU.mult, op1=ALU.add).then_inc(table_v, 1)

            take(NCH - 1, (NCH - 1) % 2)
            codes_of_pairs()
            prepare(NCH - 1)

            def split_q(u, late=False):
                buf = [q_raw(u, f, late).rearrange("p (t i) -> p t i", t=TG) for f in range(H)]
                part = [[q_hl[:, bass.ds(u * TG, TG), f, a, :] for a in range(2)] for f in range(H)]
                for f in range(H):
                    dve.wait_ge(q_f, 2 * u + f + 3)
                    V.tensor_scalar(part[f][0], buf[f], 1.0, None, ALU.mult).then_inc(q_split, 1)
                for f in range(H):
                    dve.wait_ge(q_split, 4 * u + f + 9)
                    V.scalar_tensor_tensor(out=part[f][1], in0=buf[f], scalar=1.0, in1=part[f][0],
                                           op0=ALU.mult, op1=ALU.subtract).then_inc(q_split, 1)

            def split_qs(first, end):
                with dve.Fori(first, end) as u:
                    split_q(u)

            split_qs(0, 3)
            dve.wait_ge(exp_done, NBLK)
            dve.wait_ge(min_done, T)
            units = nm_q[:, :].rearrange("p (t u) -> p t u", u=U)
            sums = z_q[:, :].rearrange("p (t u) -> p t u", u=U)
            V.tensor_reduce(nm_all[:, 0:T], units, AX.X, ALU.min).then_inc(state_v, 1)
            dve.wait_ge(state_v, 1)
            V.tensor_tensor(units, nm_all[:, 0:T].rearrange("p (t o) -> p t o", o=1).to_broadcast([P, T, U]), units,
                            ALU.subtract).then_inc(state_v, 1)
            dve.wait_ge(code_mm, 1)
            dve.wait_ge(z_kept, NCH)
            step(V.tensor_copy(crow, bank[2][0:1, 0:NT * P]))
            V.scalar_tensor_tensor(out=tab_pe, in0=crow[:, 2:NTAB + 2], scalar=512.0, in1=crow[:, 0:NTAB],
                                   op0=ALU.mult, op1=ALU.add)
            V.scalar_tensor_tensor(out=tab_dve[:, 1:NTAB], in0=crow[:, 3:NTAB + 2], scalar=512.0,
                                   in1=crow[:, 0:NTAB - 1], op0=ALU.mult, op1=ALU.add)
            V.tensor_scalar(tab_dve[:, 0:1], crow[:, 2:3], 512.0, 8.0 * T, ALU.mult, ALU.add)
            step(V.tensor_scalar(npairs, incl[0:1, T - 1:T], -1.0, None, ALU.add))
            dve.sem_inc(table_done, 1)
            split_qs(3, NCH - 2)
            dve.wait_ge(state_a, 1)
            step(V.tensor_tensor(z_q[:, :], z_q[:, :], nm_q[:, :], ALU.mult))
            step(V.tensor_reduce(z_all[:, :], sums, AX.X, ALU.add))
            dve.wait_ge(o_zero, 1)
            V.tensor_scalar(o_all[:, 0:T, D], z_all[:, :], SP * SV, None, ALU.mult).then_inc(o_ready, 1)
            step(V.memset(alpha[:, 0:1], 1.0))
            dve.wait_ge(c_done, T)
            step(V.tensor_tensor(nm_all[:, 0:T], nm_all[:, 0:T], c_all[:, :], ALU.add))
            nr1 = rounds(dve)
            first_codes = codes(dve, DVE_E, tab_pe, 0)
            dve.wait_ge(q_split, 4 * (NCH - 2) + 8)

            def score(f, tt, sl, loads):
                tile, chunk = f
                s = sl % 2
                later = not isinstance(tt, int)
                if later:
                    dve.wait_ge(alpha_done, tt - 1)
                if later or tt:
                    dve.wait_ge(nm_kept, tt)
                V.tensor_scalar(pre[:, s:s + 1], nm_all[:, bass.ds(tile, 1)], 1.0, None, ALU.mult).then_inc(pre_done, 1)
                dve.wait_ge(sc_mm, tt + 1)
                dve.wait_ge(adj_in[sl], 16 * loads)
                V.scalar_tensor_tensor(out=adjc[sl], in0=adjc[sl], scalar=-2.0 * KS, in1=bank[s][:, :],
                                       op0=ALU.mult, op1=ALU.subtract).then_inc(sc_read, 1)
                waits = [(pre_done, tt + 1), (pen1_done, tt + 1), (sc_read, tt + 1)]
                if later:
                    waits.append((tr_mm, tt - 1))
                wait_apart(dve, *waits)
                V.tensor_tensor_reduce(prob[s], adjc[sl], pen1[s], 1.0 / KS, pre[:, s:s + 1], ALU.add, ALU.min,
                                       nnew[:, s:s + 1]).then_inc(tsc_done, 1)

            def keep_max(tile, tt, s):
                dve.wait_ge(tsc_done, tt + 1)
                V.tensor_scalar(nm_all[:, bass.ds(tile, 1)], nnew[:, s:s + 1], 1.0, None, ALU.mult).then_inc(nm_kept, 1)

            def gather(tile, after, s):
                al = alpha[:, bass.ds(after, 1)]
                dve.wait_ge(pv_mm, after + 1)
                dve.wait_ge(o_done, after + 1)
                o = o_all[:, bass.ds(tile, 1), :].rearrange("p o d -> p (o d)")
                V.scalar_tensor_tensor(out=o, in0=o, scalar=al, in1=bank[6 + s][:, 0:D + 1],
                                       op0=ALU.mult, op1=ALU.add).then_inc(o_done, 1)

            dve.wait_ge(o_ready, 1)
            dve.sem_inc(o_done, 1)
            dve.sem_inc(pt_lo, 1)
            dve.sem_inc(pv_mm, 1)
            for s in range(2):
                f = fields(dve, first_codes[s], 0)
                score(f, s, s, 1)
                keep_max(f[0], s, s)
                if s == 0:
                    split_q(NCH - 2, late=True)
            split_q(NCH - 1, late=True)
            with dve.Fori(0, nr1 + 1) as r:
                v = codes(dve, DVE_E, tab_dve, r)
                for k in range(ROUND):
                    s = k % 2
                    tt = ROUND * r + k
                    ahead = fields(dve, v[k], 9)
                    dve.wait_ge(pt_hi, tt + 1)
                    V.scalar_tensor_tensor(out=pt[s][:, CW:2 * CW], in0=bank[2 + s][:, :], scalar=SP,
                                           in1=pt[s][:, 0:CW], op0=ALU.mult, op1=ALU.subtract).then_inc(pt_lo, 1)
                    score(ahead, tt + 2, (k + 2) % 4, ROUND // 4 * r + (k + 2) // 4 + 1)
                    gather(fields(dve, v[k], 0)[0], tt, 1 - s)
                    keep_max(ahead[0], tt + 2, s)
            v = codes(dve, DVE_E, tab_dve, nr1 + 1)
            gather(fields(dve, v[0], 0)[0], ROUND * (nr1 + 1), 1)

            dve.wait_ge(alpha_done, ROUND * nr1 + ROUND + 1)
            dve.wait_ge(o_done, ROUND * nr1 + ROUND + 2)
            V.reciprocal(rz[:, :], o_all[:, 0:T, D]).then_inc(rz_done, 1)
            dve.wait_ge(rz_done, 1)

            def stats(g):
                now = slice(g * TG, (g + 1) * TG)
                dve.wait_ge(sdf_done, g + 1)
                V.reciprocal(rstdf[:, now], rstdf[:, now]).then_inc(statf_done, 1)
                dve.wait_ge(statf_done, 2 * g + 1)
                V.scalar_tensor_tensor(out=shiftf[:, now], in0=mvf[:, now, 0], scalar=-1.0, in1=rstdf[:, now],
                                       op0=ALU.mult, op1=ALU.mult).then_inc(statf_done, 1)

            for g in range(NCH):
                tiles = range(g * TG, (g + 1) * TG)
                for i in tiles[0:TG - 2]:
                    V.scalar_tensor_tensor(out=o_all[:, i, 0:D], in0=o_all[:, i, 0:D], scalar=rz[:, i:i + 1],
                                           in1=z[:, i, :], op0=ALU.mult, op1=ALU.add).then_inc(x2_done, 1)
                for i in tiles:
                    dve.wait_ge(x2_done if i % TG < 2 else x2_pool, 2 * g + i % 2 + 1)
                    V.bn_stats(bnf[:, i, :], o_all[:, i, 0:D]).then_inc(bnf_done, 1)
                for i in tiles:
                    dve.wait_ge(bnf_done, i + 1)
                    last = V.bn_aggr(mvf[:, i, :], bnf[:, i, :])
                last.then_inc(var_done, 1)
                if g:
                    stats(g - 1)
            stats(NCH - 1)
            dve.wait_ge(statf_done, 2 * NCH)
            for i in range(T - 2, T):
                V.tensor_scalar(o_all[:, i, 0:D], o_all[:, i, 0:D], mvf[:, i, 0:1], rstdf[:, i:i + 1],
                                ALU.subtract, ALU.mult).then_inc(y_last, 1)


def kernel(**inputs):
    import numpy as np
    import concourse.bacc as bacc
    from concourse.bass_utils import run_bass_kernel_spmd

    nc = bacc.Bacc("TRN2", target_bir_lowering=False, num_devices=1)
    host = {k: np.asarray(v) for k, v in inputs.items()}
    layout = {
        "x": host["x"],
        "xT": host["x"].T,
        "adj": host["adj"],
        "adjT": host["adj"].T,
        "t": host["L0_gnn_t"],
        "W": host["L0_gnn_weight"],
        "ptr": host["L1_gnn_ptr"],
        "Wq": host["L1_gnn_Wq"],
        "bq": host["L1_gnn_bq"],
        "Wk": host["L1_gnn_Wk"],
        "bk": host["L1_gnn_bk"],
        "WvT": host["L1_gnn_Wv"].T,
        "bv": host["L1_gnn_bv"],
    }
    arrays, args = {}, []
    for name, a in layout.items():
        a = np.ascontiguousarray(a)
        arrays[f"in_{name}"] = a
        args.append(nc.dram_tensor(f"in_{name}", a.shape, mybir.dt.from_np(a.dtype), kind="ExternalInput").ap())
    shape = host["x"].shape
    out = nc.dram_tensor("out_y", shape, F32, kind="ExternalOutput").ap()
    build(nc, *args, out)
    r = run_bass_kernel_spmd(nc, [arrays], core_ids=[0])
    return r.results[0]["out_y"]
```
